# Optimizing a Trainium2 kernel written in Bass

```python
import numpy as np
import jax
import jax.numpy as jnp

def _softmax(x, axis=-1):
    return jax.nn.softmax(x, axis=axis)

def _gelu(x):
    return jax.nn.gelu(x, approximate=True)

def _silu(x):
    return jax.nn.silu(x)

def _sigmoid(x):
    return jax.nn.sigmoid(x)

def _layernorm(x, axis=-1, eps=1e-05):
    m = jnp.mean(x, axis=axis, keepdims=True)
    v = jnp.var(x, axis=axis, keepdims=True)
    return (x - m) / jnp.sqrt(v + eps)

def _scatter_add(tgt, idx, src, axis=0):
    return tgt.at[idx].add(src)

def _segment_sum(src, seg, n):
    return jax.ops.segment_sum(src, seg, n)
kernel_name = 'mk_adj_resnorm_d4_adj_r2_89043f'

def setup_inputs(seed: int=0):
    np.random.seed(seed)
    _w = jnp.asarray

    def _rec_inputs():
        import jax
        import jax.numpy as jnp
        _gk = jax.random.key(seed)
        x = -0.0002928 + 1 * jax.random.normal(jax.random.fold_in(_gk, 1), (16, 512, 128), jnp.float32)
        _w = (1.0 + jnp.arange(512, dtype=jnp.float32)) ** (-0.5)
        _w = _w / _w.mean()
        _pij = jnp.clip(0.03125 * _w[:, None] * _w[None, :], 0.0, 1.0)
        _a = jax.random.uniform(jax.random.fold_in(_gk, 2), (16, 512, 512)) < _pij
        adj = _a.astype(jnp.int32)
        return (x, adj)
    x, adj = _rec_inputs()

    def _L0_gnn_setup():
        import jax, jax.numpy as jnp
        import numpy as np
        NEG_INF = -1000000000.0
        LEAKY_SLOPE = 0.2
        key = jax.random.key(seed)
        k1, k2, k3, k4 = jax.random.split(key, 4)
        B, N, D_in, D_out = (8, 1024, 128, 128)
        x = jax.random.normal(k1, (B, N, D_in), dtype=jnp.float32)
        adj_matrix = jax.random.randint(k2, (B, N, N), 0, 2, dtype=jnp.int32)
        W = jax.random.normal(k3, (D_out, D_in), dtype=jnp.float32) / np.sqrt(D_in)
        a = jax.random.normal(k4, (1, 2 * D_out), dtype=jnp.float32) / np.sqrt(2 * D_out)
        return {'x': x, 'adj_matrix': adj_matrix, 'W': W, 'a': a}
    _L0_gnn_all = _L0_gnn_setup()
    _L0_gnn_in = {k: v for k, v in _L0_gnn_all.items() if k in ('W', 'a')}
    del _L0_gnn_all

    def _L1_gnn_setup():
        import jax, jax.numpy as jnp
        import numpy as np
        B, N, F_IN, F_OUT = (8, 1024, 128, 128)
        ALPHA = 0.2
        NEG_BIG = -9000000000000000.0
        key = jax.random.key(seed)
        k1, k2, k3, k4 = jax.random.split(key, 4)
        x = jax.random.normal(k1, (B, N, F_IN), dtype=jnp.float32)
        adj = jax.random.randint(k2, (B, N, N), 0, 2, dtype=jnp.int32)
        gain = 1.414
        lim_W = gain * np.sqrt(6.0 / (F_IN + F_OUT))
        W = jax.random.uniform(k3, (F_IN, F_OUT), dtype=jnp.float32, minval=-lim_W, maxval=lim_W)
        lim_a = gain * np.sqrt(6.0 / (2 * F_OUT + 1))
        a = jax.random.uniform(k4, (2 * F_OUT, 1), dtype=jnp.float32, minval=-lim_a, maxval=lim_a)
        return {'x': x, 'adj': adj, 'W': W, 'a': a}
    _L1_gnn_all = _L1_gnn_setup()
    _L1_gnn_in = {k: v for k, v in _L1_gnn_all.items() if k in ('W', 'a')}
    del _L1_gnn_all

    def _L2_gnn_setup():
        import jax, jax.numpy as jnp
        import numpy as np
        B, N, IN_F, OUT_F = (8, 1024, 128, 128)
        ALPHA = 0.2
        NEG_INF = -1000000000.0
        key = jax.random.key(seed)
        ks = jax.random.split(key, 8)
        h = jax.random.normal(ks[0], (B, N, IN_F), dtype=jnp.float32)
        adj = jax.random.randint(ks[1], (B, N, N), 0, 2, dtype=jnp.int32)
        W_w = jax.random.normal(ks[2], (OUT_F, IN_F), dtype=jnp.float32) * (1.414 / np.sqrt(IN_F + OUT_F))
        W_b = jnp.zeros((OUT_F,), dtype=jnp.float32)
        ai_w = jax.random.normal(ks[3], (1, OUT_F), dtype=jnp.float32) * (1.414 / np.sqrt(OUT_F + 1))
        ai_b = jnp.zeros((1,), dtype=jnp.float32)
        aj_w = jax.random.normal(ks[4], (1, OUT_F), dtype=jnp.float32) * (1.414 / np.sqrt(OUT_F + 1))
        aj_b = jnp.zeros((1,), dtype=jnp.float32)
        return {'h': h, 'adj': adj, 'W_w': W_w, 'W_b': W_b, 'ai_w': ai_w, 'ai_b': ai_b, 'aj_w': aj_w, 'aj_b': aj_b}
    _L2_gnn_all = _L2_gnn_setup()
    _L2_gnn_in = {k: v for k, v in _L2_gnn_all.items() if k in ('W_w', 'W_b', 'ai_w', 'ai_b', 'aj_w', 'aj_b')}
    del _L2_gnn_all

    def _L3_gnn_setup():
        import jax, jax.numpy as jnp
        import numpy as np
        B, N, D_IN, D_OUT, R = (8, 1024, 128, 128, 4)
        key = jax.random.key(seed)
        k1, k2, k3, k4 = jax.random.split(key, 4)
        x = jax.random.normal(k1, (B, N, D_IN), dtype=jnp.float32)
        adj = jnp.zeros((1,), dtype=jnp.float32)
        relation = jax.random.randint(k2, (B, N, N), 0, R + 1, dtype=jnp.int32)
        weight = jax.random.normal(k3, (R, D_IN, D_OUT), dtype=jnp.float32) * 0.05
        bias = jax.random.normal(k4, (D_OUT,), dtype=jnp.float32) * 0.05
        return {'x': x, 'adj': adj, 'relation': relation, 'weight': weight, 'bias': bias}
    _L3_gnn_all = _L3_gnn_setup()
    _L3_gnn_in = {k: v for k, v in _L3_gnn_all.items() if k in ('adj', 'weight', 'bias')}
    del _L3_gnn_all
    return {'x': x, 'adj': adj, 'L0_gnn_W': _L0_gnn_in['W'], 'L0_gnn_a': _L0_gnn_in['a'], 'L1_gnn_W': _L1_gnn_in['W'], 'L1_gnn_a': _L1_gnn_in['a'], 'L2_gnn_W_w': _L2_gnn_in['W_w'], 'L2_gnn_W_b': _L2_gnn_in['W_b'], 'L2_gnn_ai_w': _L2_gnn_in['ai_w'], 'L2_gnn_ai_b': _L2_gnn_in['ai_b'], 'L2_gnn_aj_w': _L2_gnn_in['aj_w'], 'L2_gnn_aj_b': _L2_gnn_in['aj_b'], 'L3_gnn_adj': _L3_gnn_in['adj'], 'L3_gnn_weight': _L3_gnn_in['weight'], 'L3_gnn_bias': _L3_gnn_in['bias']}

def reference(x, adj, L0_gnn_W, L0_gnn_a, L1_gnn_W, L1_gnn_a, L2_gnn_W_w, L2_gnn_W_b, L2_gnn_ai_w, L2_gnn_ai_b, L2_gnn_aj_w, L2_gnn_aj_b, L3_gnn_adj, L3_gnn_weight, L3_gnn_bias):
    import jax
    import jax.numpy as jnp

    def _L0_gnn_ref(x, adj_matrix, W, a):
        import jax, jax.numpy as jnp
        import numpy as np
        NEG_INF = -1000000000.0
        LEAKY_SLOPE = 0.2
        h = jnp.einsum('bnd,od->bno', x, W)
        D = h.shape[-1]
        a_left, a_right = (a[0, :D], a[0, D:])
        e = (h @ a_left)[:, :, None] + (h @ a_right)[:, None, :]
        e = jnp.where(e > 0, e, LEAKY_SLOPE * e)
        e = jnp.where(adj_matrix == 0, NEG_INF, e)
        alpha = jax.nn.softmax(e, axis=-1)
        return jnp.einsum('bij,bjd->bid', alpha, h)

    def _L1_gnn_ref(x, adj, W, a):
        import jax, jax.numpy as jnp
        import numpy as np
        B, N, F_IN, F_OUT = (8, 1024, 128, 128)
        ALPHA = 0.2
        NEG_BIG = -9000000000000000.0
        h = jnp.einsum('bnf,fo->bno', x, W)
        a1 = a[:F_OUT, 0]
        a2 = a[F_OUT:, 0]
        s1 = h @ a1
        s2 = h @ a2
        e = jax.nn.leaky_relu(s1[:, :, None] + s2[:, None, :], negative_slope=ALPHA)
        att = jnp.where(adj > 0, e, jnp.float32(NEG_BIG))
        att = jax.nn.softmax(att, axis=1)
        h_prime = jnp.einsum('bij,bjo->bio', att, h)
        return jax.nn.elu(h_prime)

    def _L2_gnn_ref(h, adj, W_w, W_b, ai_w, ai_b, aj_w, aj_b):
        import jax, jax.numpy as jnp
        import numpy as np
        B, N, IN_F, OUT_F = (8, 1024, 128, 128)
        ALPHA = 0.2
        NEG_INF = -1000000000.0
        Wh = jnp.einsum('bni,oi->bno', h, W_w) + W_b
        Wh1 = jnp.einsum('bnf,of->bno', Wh, ai_w) + ai_b
        Wh2 = jnp.einsum('bnf,of->bno', Wh, aj_w) + aj_b
        e = Wh1 + jnp.swapaxes(Wh2, 1, 2)
        e = jnp.where(e >= 0, e, ALPHA * e)
        attention = jnp.where(adj > 0, e, NEG_INF)
        attention = jax.nn.softmax(attention, axis=2)
        h_hat = jnp.einsum('bnm,bmf->bnf', attention, Wh)
        return jax.nn.elu(h_hat)

    def _L3_gnn_ref(x, adj, relation, weight, bias):
        import jax, jax.numpy as jnp
        import numpy as np
        B, N, D_IN, D_OUT, R = (8, 1024, 128, 128, 4)
        rel_ids = jnp.arange(1, weight.shape[0] + 1, dtype=relation.dtype)
        masks = (relation[None] == rel_ids[:, None, None, None]).astype(x.dtype)
        h = jnp.einsum('rbnm,bmd->rbnd', masks, x)
        y = jnp.einsum('rbnd,rdo->bno', h, weight)
        return y + bias
    x = _layernorm(x + _L0_gnn_ref(x, adj, L0_gnn_W, L0_gnn_a), axis=-1)
    x = _layernorm(x + _L1_gnn_ref(x, adj, L1_gnn_W, L1_gnn_a), axis=-1)
    x = _layernorm(x + _L2_gnn_ref(x, adj, L2_gnn_W_w, L2_gnn_W_b, L2_gnn_ai_w, L2_gnn_ai_b, L2_gnn_aj_w, L2_gnn_aj_b), axis=-1)
    x = _layernorm(x + _L3_gnn_ref(x, L3_gnn_adj, adj, L3_gnn_weight, L3_gnn_bias), axis=-1)
    return x

_drawn_inputs = setup_inputs


def setup_inputs(seed=0):
    import zlib

    import numpy as np

    out = dict(_drawn_inputs(seed))
    spreads = {'L2_gnn_W_b': (0.0, 0.1)}
    factors = {'L3_gnn_bias': 4.1}
    for name, (base, spread) in spreads.items():
        noise = np.random.default_rng([zlib.crc32(name.encode()), seed]).standard_normal(out[name].shape)
        drawn = base * np.exp(spread * noise) if base else spread * noise
        out[name] = jnp.asarray(drawn.astype(out[name].dtype))
    for name, factor in factors.items():
        out[name] = (out[name] * factor).astype(out[name].dtype)
    return out
```

```python
from contextlib import ExitStack

import concourse.bass as bass
from concourse import mybir

F32 = mybir.dt.float32
BF16 = mybir.dt.bfloat16
I32 = mybir.dt.int32
ALU = mybir.AluOpType
ACT = mybir.ActivationFunctionType
AX = mybir.AxisListType

P = 128
G = 16
N = 512
D = 128
C = N // P
REL = 4
EPS = 1e-5
SLOPE = 0.2
R_MAX = 5.5e34
TINY = 1e-37
LAYERS = 3
UNROLL = 4
S1, S2, DEG = 129, 130, 131
LOOP0, LOOP1 = 1, 13
TILT, FULL, BIAS, Z, RZ = 3, 4, 5, 6, 7


class Item:

    def __init__(self, l, g, r):
        self.l, self.g, self.r, self.b = l, g, r % 4, r % 2
        self.done = g + (G * l + 1)
        self.of_layer = g + 1


def item(n):
    return Item(n // G, n % G, n % G) if n >= 0 else None


def build(nc, x, adj, adj_rows, w0, w0t, a0, w1, w1t, a1, w2, w2t, a2, b2, ab2, w3, b3, out):
    ctx = ExitStack()
    with ctx:
        def sb(name, shape, dt=F32):
            return ctx.enter_context(nc.sbuf_tensor(name, shape, dt))

        def pb(name, shape, dt=F32):
            return ctx.enter_context(nc.psum_tensor(name, shape, dt))

        sems = {}

        def sem(name):
            if name not in sems:
                sems[name] = ctx.enter_context(nc.semaphore(name))
            return sems[name]

        X = sb("X", [P, G, C, D])
        MT = sb("MT", [P, G, C, N], BF16)
        adj_in = sb("adj_in", [P, 2, C, N], I32)
        square_out = sb("square_out", [P, C * N], BF16)
        flag_sum = sb("flag_sum", [P, G, 1])
        empty_row = sb("empty_row", [P, G, C])
        empty_col = sb("empty_col", [P, G, C])
        x_cur = sb("x_cur", [P, 2, C, D])
        xT = sb("xT", [P, 2, N])
        x_sum = sb("x_sum", [P, 2])
        hx = sb("hx", [P, 4, C, 132])
        h_mean = sb("h_mean", [P, 2, D])
        h_scaled = sb("h_scaled", [P, 2, C, D])
        smax_own = sb("smax_own", [P, 2])
        smax = sb("smax", [P, 2])
        shifts = sb("shifts", [P, 2, 3])
        factors_raw = sb("factors_raw", [P, 2, 3, C])
        factors = sb("factors", [P, 2, 3, C])
        neg_d = sb("neg_d", [P, 2, C])
        q_rows = sb("q_rows", [P, 2, N])
        edge = sb("edge", [P, C, N])
        PT = sb("PT", [P, 2, C, N])
        col_tmp = sb("col_tmp", [P, 2, 8, C])
        residual = sb("residual", [P, 2, C, D])
        mean_term = sb("mean_term", [P, 2, C, D])
        z_row = sb("z_row", [P, 2, C])
        rz_row = sb("rz_row", [P, 2, C])
        y = sb("y", [P, 2, C, D])
        elu_exp = sb("elu_exp", [P, C, D])
        stats = sb("stats", [P, C, 6])
        mean_var = sb("mean_var", [P, 2, C, 2])
        var_eps = sb("var_eps", [P, 2, C])
        rstd = sb("rstd", [P, 2, C])
        split = sb("split", [P, 4, 3, C, D], BF16)
        rest = sb("rest", [P, C, D])
        ident = sb("ident", [P, P])
        ones_bf = sb("ones_bf", [P, 1], BF16)
        col_sum = sb("col_sum", [P, 2, C])
        count = sb("count", [P, 2, C])
        flag_own = sb("flag_own", [P, 2])
        neg_half = sb("neg_half", [P, C])
        eps_tile = sb("eps_tile", [P, C])
        minus_one = sb("minus_one", [P, C])
        minus_half = sb("minus_half", [P, 1])
        wx = sb("wx", [P, 3, 130])
        w_back = sb("w_back", [P, 3, D])
        a_cols = sb("a_cols", [P, 3, 2])
        w_rel = sb("w_rel", [P, REL, D])
        bias2 = sb("bias2", [P, D])
        bias2_col = sb("bias2_col", [P, 1])
        bias3 = sb("bias3", [P, D])
        ab2_sb = sb("ab2_sb", [P, 2])
        shift_k = sb("shift_k", [P, 3])
        b2_a = sb("b2_a", [P, 2])
        b2_ab = sb("b2_ab", [P, 2])
        shift_add = sb("shift_add", [P, LAYERS, 3])
        flag_int = sb("flag_int", [P, 1], I32)

        xT_ps = pb("xT_ps", [P, N])
        h_ps = pb("h_ps", [P, C, 256])
        rows_ps = pb("rows_ps", [P, N])
        o_ps = [pb(f"o_ps{b}", [P, C, 256]) for b in range(2)]
        h_mean_ps = h_ps[:, 2:4, 132:196]
        smax_ps = h_ps[:, 0:2, 132:196]

        block = ctx.enter_context(nc.Block())

        def pipeline(eng, slot, first, layers):
            last = first + G * layers
            n = first - 3
            while n <= last:
                if n >= first and n % G == LOOP0:
                    l = n // G
                    with eng.Fori(LOOP0, LOOP1 - UNROLL + 1, UNROLL) as i:
                        for u in range(UNROLL):
                            slot(lambda k, u=u: Item(l, i + (u + k), LOOP0 + u + k + 4), None)
                    n += LOOP1 - LOOP0
                else:
                    slot(lambda k, n=n: item(n + k) if first <= n + k < last else None, n)
                    n += 1

        def halves(it):
            return it.of_layer + (G if it.l == 2 else 0)

        def landed(it):
            return 16 * (it.g // 4 + 1) if isinstance(it.g, int) else it.g * 4 + (16 - 4 * it.r)

        def settle(eng):
            eng.wait_ge(sem("ready"), 1)

        def not_binary(eng):
            eng.wait_ge(sem("flag"), 1)
            return eng.value_load(flag_int[0:1, 0:1], min_val=0, max_val=1) > 0

        @block.sync
        def _(sp):
            for l, (w, wb, a) in enumerate(((w0t, w0, a0), (w1, w1t, a1), (w2t, w2, a2))):
                sp.dma_start(wx[:, l, 0:D], w).then_inc(sem("w_in"), 16)
                sp.dma_start(w_back[:, l, :], wb).then_inc(sem("w_in"), 16)
                sp.dma_start(a_cols[:, l, :], a).then_inc(sem("w_in"), 16)
            sp.dma_start(bias2_col[:, :], b2.rearrange("(p o) -> p o", o=1)).then_inc(sem("w_in"), 16)
            sp.dma_start(bias2[:, :], b2.partition_broadcast(P)).then_inc(sem("w_in"), 16)
            sp.dma_start(ab2_sb[:, :], ab2.partition_broadcast(P)).then_inc(sem("w_in"), 16)

            def load(it):
                settle(sp)
                if not isinstance(it.g, int) or it.g >= 2:
                    sp.wait_ge(sem("mask"), it.of_layer - 2)
                    sp.wait_ge(sem("flag_sum"), it.of_layer - 2)
                sp.dma_start(adj_in[:, it.b, :, :], adj[it.g, :, :, :]).then_inc(sem(f"adj_in{it.r}"), 16)

            for n in range(4):
                sp.dma_start(X[:, 4 * n:4 * n + 4, :, :], x[4 * n:4 * n + 4, :, :, :].rearrange("g p c d -> p g c d"))\
                    .then_inc(sem(f"x_in{n}"), 16)
                load(item(n))
            sp.dma_start(w_rel[:, :, :], w3.rearrange("r d o -> d r o")).then_inc(sem("w_late"), 16)
            sp.dma_start(bias3[:, :], b3.partition_broadcast(P)).then_inc(sem("w_late"), 16)
            with sp.Fori(4, G - UNROLL + 1, UNROLL) as i:
                for u in range(UNROLL):
                    load(Item(0, i + u, u))

            with sp.If(not_binary(sp)):
                with sp.Fori(0, G) as g:
                    settle(sp)
                    sp.wait_ge(sem("rebuild_taken"), g + 1)
                    sp.dma_start(adj_in[:, 0, :, :], adj[g, :, :, :]).then_inc(sem("rebuild_in"), 16)
                    sp.dma_start(adj_in[:, 1, :, :], adj_rows[g, :, :, :]).then_inc(sem("rebuild_in"), 16)
                with sp.Fori(0, G) as g:
                    settle(sp)
                    sp.wait_ge(sem("rel_adj_free"), g + 1)
                    sp.dma_start(adj_in[:, 0, :, :], adj[g, :, :, :]).then_inc(sem("rel_adj_in"), 16)
                with sp.Fori(0, G) as g:
                    settle(sp)
                    sp.wait_ge(sem("rel_x_new"), g + 2)
                    sp.dma_start(out[g, :, :, :], X[:, g, :, :]).then_inc(sem("rel_out"), 16)
                sp.wait_ge(sem("rel_out"), 16 * G)
            with sp.Else():
                with sp.Fori(0, G) as g:
                    settle(sp)
                    sp.wait_ge(sem("x_new"), g + (G * LAYERS + 1))
                    sp.dma_start(out[g, :, :, :], X[:, g, :, :]).then_inc(sem("out"), 16)
                sp.wait_ge(sem("out"), 16 * G)

        W_IN = 16 * 12

        @block.gpsimd
        def _(pool):
            pool.memset(ident[:], 0.0).then_inc(sem("ident_zero"), 1)
            pool.wait_ge(sem("ident_zero"), 1)
            pool.affine_select(out=ident[:], in_=ident[:], compare_op=ALU.not_equal, fill=1.0, base=0,
                               pattern=[[-1, P]], channel_multiplier=1).then_inc(sem("ident"), 1)
            pool.memset(neg_half[:], -0.5)
            pool.memset(eps_tile[:], EPS)
            pool.memset(minus_one[:], -1.0).then_inc(sem("pool_const"), 1)
            pool.wait_ge(sem("pool_const"), 1)

            def copy_x(it):
                if it.l == 0:
                    for quarter in range(4) if not isinstance(it.g, int) or it.g >= 4 else (0,):
                        pool.wait_ge(sem(f"x_in{quarter}"), 16)
                else:
                    pool.wait_ge(sem("x_new"), it.done - G)
                if not isinstance(it.g, int) or it.l > 0 or it.g >= 2:
                    pool.wait_ge(sem("xT_ps"), it.done - 2)
                pool.tensor_copy(x_cur[:, it.b, :, :], X[:, it.g, :, :]).then_inc(sem("x_cur"), 1)

            def mean_and_residual(it):
                xg = X[:, it.g, :, :]
                settle(pool)
                if not isinstance(it.g, int) or it.l > 0 or it.g >= 2:
                    pool.wait_ge(sem("y_sum"), it.done - 2)
                if it.l in (0, 2):
                    pool.wait_ge(sem("h_mean"), halves(it))
                    if it.l == 0:
                        pool.wait_ge(sem("empty_row"), it.of_layer)
                    pool.tensor_tensor(mean_term[:, it.b, :, :],
                                       h_mean[:, it.b, :].unsqueeze(1).broadcast_to([P, C, D]),
                                       empty_row[:, it.g, :].unsqueeze(2).broadcast_to([P, C, D]),
                                       ALU.mult).then_inc(sem("mean_raw"), 1)
                    settle(pool)
                    pool.wait_ge(sem("mean_raw"), halves(it))
                if it.l == 0:
                    pool.tensor_tensor(residual[:, it.b, :, :], xg, mean_term[:, it.b, :, :],
                                       ALU.add).then_inc(sem("residual"), 1)
                    return
                if it.l == 2:
                    pool.tensor_tensor(mean_term[:, it.b, :, :], mean_term[:, it.b, :, :],
                                       bias2[:, :].unsqueeze(1).broadcast_to([P, C, D]),
                                       ALU.add).then_inc(sem("mean_term"), 1)
                pool.tensor_tensor(residual[:, it.b, :, :], xg, minus_one[:, :].unsqueeze(2).broadcast_to([P, C, D]),
                                   ALU.add).then_inc(sem("residual"), 1)

            def scale_h(it):
                pool.wait_ge(sem("rz_col"), it.of_layer)
                pool.wait_ge(sem("att"), it.done - 2)
                pool.tensor_tensor(h_scaled[:, it.b, :, :], hx[:, it.r, :, 1:1 + D],
                                   col_tmp[:, it.b, RZ, :].unsqueeze(2).broadcast_to([P, C, D]),
                                   ALU.mult).then_inc(sem("h_scaled"), 1)

            def rsqrt(b, mean_var_sem, names, done):
                pool.wait_ge(mean_var_sem, done)
                pool.tensor_tensor(var_eps[:, b, :], mean_var[:, b, :, 1], eps_tile[:], ALU.add)\
                    .then_inc(sem(names[0]), 1)
                pool.wait_ge(sem(names[0]), done)
                pool.tensor_tensor(rstd[:, b, :], var_eps[:, b, :], neg_half[:], ALU.pow)\
                    .then_inc(sem(names[1]), 1)

            def attention_slot(at, n):
                if at(3):
                    copy_x(at(3))
                if at(1) and at(1).l == 1:
                    scale_h(at(1))
                if at(1):
                    mean_and_residual(at(1))
                if at(-1):
                    rsqrt(at(-1).b, sem("mean_var"), ("var_eps", "rstd"), at(-1).done)

            def relation_slot(at, n):
                if at(3):
                    copy_x(at(3))
                if at(1):
                    it = at(1)
                    settle(pool)
                    pool.wait_ge(sem("y_sum"), it.done - 2)
                    pool.tensor_tensor(residual[:, it.b, :, :], X[:, it.g, :, :],
                                       bias3[:, :].unsqueeze(1).broadcast_to([P, C, D]),
                                       ALU.add).then_inc(sem("residual"), 1)
                if at(-1):
                    rsqrt(at(-1).b, sem("mean_var"), ("var_eps", "rstd"), at(-1).done)

            pipeline(pool, attention_slot, 0, LAYERS)
            pool.wait_ge(sem("w_late"), 32)
            with pool.If(not_binary(pool)):
                with pool.Fori(0, G) as g:
                    pool.wait_ge(sem("x_new"), g + (G * 2 + 1))
                    pool.wait_ge(sem("rel_x_new"), g + 1)
                    pool.tensor_copy(x_cur[:, 0, :, :], X[:, g, :, :]).then_inc(sem("rel_x_cur"), 1)
                    pool.tensor_tensor(residual[:, 0, :, :], X[:, g, :, :],
                                       bias3[:, :].unsqueeze(1).broadcast_to([P, C, D]),
                                       ALU.add).then_inc(sem("rel_residual"), 1)
                    rsqrt(0, sem("rel_mean_var"), ("rel_var_eps", "rel_rstd"), g + 1)
            with pool.Else():
                pipeline(pool, relation_slot, G * LAYERS, 1)

        @block.tensor
        def _(pe):
            pe.wait_ge(sem("w_in"), W_IN)
            for l in range(LAYERS):
                pe.matmul(xT_ps[:, 2 * l:2 * l + 2], w_back[:, l, :], a_cols[:, l, :], start=True, stop=True)
            pe.matmul(xT_ps[:, 6:8], bias2_col[:, 0:1].broadcast_to([P, P]), a_cols[:, 2, :],
                      start=True, stop=True).then_inc(sem("wa_ps"), 1)
            pe.wait_ge(sem("ident"), 1)
            pe.wait_ge(sem("wa"), 1)
            pe.wait_ge(sem("ones"), 1)

            def transpose_x(x_sem, done, b):
                pe.wait_ge(x_sem, done)
                for c in range(C):
                    last = pe.transpose(xT_ps[:, c * P:(c + 1) * P], x_cur[:, b, c, :], ident[:])
                return last

            def next_transpose(it):
                if not isinstance(it.g, int) or it.l > 0 or it.g >= 1:
                    pe.wait_ge(sem("xT"), it.done - 1)
                transpose_x(sem("x_cur"), it.done, it.b).then_inc(sem("xT_ps"), 1)

            def project(it):
                pe.wait_ge(sem("xT"), it.done)
                if it.l < LAYERS:
                    if not isinstance(it.g, int) or it.l > 0 or it.g >= 1:
                        pe.wait_ge(sem("hx"), it.done - 1)
                        pe.wait_ge(sem("smax"), it.done - 1)
                elif not isinstance(it.g, int) or it.g >= 1:
                    pe.wait_ge(sem("split_rest"), it.of_layer - 1)
                if it.l == 0:
                    pe.wait_ge(sem("mask"), it.of_layer)
                for c in range(C):
                    lhsT = xT[:, it.b, c * P:(c + 1) * P]
                    if it.l < LAYERS:
                        last = pe.matmul(h_ps[:, c, 0:130], lhsT, wx[:, it.l, :], start=True, stop=True)
                    else:
                        last = pe.matmul(h_ps[:, c, 0:D], lhsT, w_rel[:, 0, :], start=True, stop=True)
                if it.l in (0, 2):
                    for e in range(2):
                        last = pe.matmul(h_mean_ps[:, e, :], x_sum[:, it.b:it.b + 1].broadcast_to([P, P]),
                                         wx[:, it.l, e * 64:(e + 1) * 64], start=True, stop=True)
                if it.l == 0:
                    for ic in range(C):
                        for jc in range(C):
                            last = pe.matmul(h_ps[:, ic, 130:131], MT[:, it.g, jc, ic * P:(ic + 1) * P],
                                             ones_bf[:, 0:1], start=(jc == 0), stop=(jc == C - 1))
                last.then_inc(sem("h_ps"), 1)

            def spread_max(it):
                pe.wait_ge(sem("smax_own"), it.done)
                pe.transpose(smax_ps, smax_own[:, it.b:it.b + 1].broadcast_to([P, P]), ident[:])\
                    .then_inc(sem("smax_ps"), 1)

            def spread_rows(it):
                if it.l == 1:
                    pe.wait_ge(sem("hx"), it.done)
                else:
                    pe.wait_ge(sem("factors"), halves(it))
                if not isinstance(it.g, int) or it.l > 0 or it.g >= 1:
                    pe.wait_ge(sem("edge"), (it.done - 1) * C)
                for c in range(C):
                    col = hx[:, it.r, c, S1:S1 + 1] if it.l == 1 else factors[:, it.b, 0, c:c + 1]
                    last = pe.transpose(rows_ps[:, c * P:(c + 1) * P], col.broadcast_to([P, P]), ident[:])
                last.then_inc(sem("rows_ps"), 1)

            def attend(it, ics):
                if ics[0] == 0:
                    pe.wait_ge(sem("PT"), it.done * C)
                    if it.l == 1:
                        pe.wait_ge(sem("h_scaled"), it.of_layer)
                for ic in ics:
                    for jc in range(C):
                        lhsT = PT[:, it.b, jc, ic * P:(ic + 1) * P]
                        if it.l == 1:
                            last = pe.matmul(o_ps[it.b][:, ic, 1:1 + D], lhsT, h_scaled[:, it.b, jc, :],
                                             start=(jc == 0), stop=(jc == C - 1))
                        else:
                            last = pe.matmul(o_ps[it.b][:, ic, 0:1 + D], lhsT, hx[:, it.r, jc, 0:1 + D],
                                             start=(jc == 0), stop=(jc == C - 1))
                if ics[-1] == C - 1:
                    last.then_inc(sem("att"), 1)

            def attention_slot(at, n):
                if at(1):
                    spread_rows(at(1))
                if at(2):
                    project(at(2))
                if n == G - 2:
                    pe.wait_ge(sem("flag_own"), 1)
                    pe.wait_ge(sem("xT"), at(2).done)
                    pe.transpose(xT_ps[:, 0:P], flag_own[:, 0:1].broadcast_to([P, P]), ident[:])\
                        .then_inc(sem("flag_ps"), 1)
                    pe.wait_ge(sem("flag_max"), 1)
                if at(3):
                    next_transpose(at(3))
                if at(0):
                    attend(at(0), (0, 1))
                if at(2):
                    spread_max(at(2))
                if at(0):
                    attend(at(0), (2, 3))

            def relate(o, g, r, first, final):
                for ic in range(C):
                    for jc in range(C):
                        for part in range(3):
                            last = pe.matmul(o[:, ic, 1:1 + D], MT[:, g, jc, ic * P:(ic + 1) * P],
                                             split[:, r, part, jc, :], start=(first and jc == 0 and part == 0),
                                             stop=(final and jc == C - 1 and part == 2),
                                             skip_group_check=not (first and final))
                return last

            def relation_slot(at, n):
                if at(2):
                    project(at(2))
                if at(3):
                    next_transpose(at(3))
                if at(0):
                    it = at(0)
                    pe.wait_ge(sem("split"), it.of_layer)
                    pe.wait_ge(sem("y_sum"), it.done - 2)
                    relate(o_ps[it.b], it.g, it.r, True, True).then_inc(sem("att"), 1)

            pipeline(pe, attention_slot, 0, LAYERS)
            pe.wait_ge(sem("w_late"), 32)
            pe.wait_ge(sem("y_sum"), G * LAYERS)
            with pe.If(not_binary(pe)):
                with pe.Fori(0, G) as g:
                    transpose_x(sem("rel_x_cur"), g + 1, 0).then_inc(sem("rel_xT_ps"), 1)
                    pe.wait_ge(sem("rel_xT"), g + 1)
                    for r in range(REL):
                        pe.wait_ge(sem("rel_split_rest"), g * REL + (r + 1))
                        for c in range(C):
                            last = pe.matmul(h_ps[:, c, 0:D], xT[:, 0, c * P:(c + 1) * P], w_rel[:, r, :],
                                             start=True, stop=True)
                        last.then_inc(sem("rel_h_ps"), 1)
                        pe.wait_ge(sem("rel_split"), g * REL + (r + 1))
                        pe.wait_ge(sem("rel_mask"), g * REL + (r + 1))
                        relate(o_ps[0], g, 0, True, True).then_inc(sem("rel_att"), 1)
            with pe.Else():
                pipeline(pe, relation_slot, G * LAYERS, 1)

        @block.scalar
        def _(act):
            act.wait_ge(sem("wa_ps"), 1)
            for l in range(LAYERS):
                act.copy(wx[:, l, D:D + 2], xT_ps[:, 2 * l:2 * l + 2])
            act.copy(b2_a[:, :], xT_ps[:, 6:8]).then_inc(sem("wa"), 1)
            act.wait_ge(sem("ones"), 1)

            def take_xT(it):
                act.wait_ge(sem("xT_ps"), it.done)
                if not isinstance(it.g, int) or it.l > 0 or it.g >= 2:
                    act.wait_ge(sem("h_ps"), it.done - 2)
                extra = dict(accum_out=x_sum[:, it.b:it.b + 1]) if it.l in (0, 2) else {}
                act.activation(xT[:, it.b, :], xT_ps[:], ACT.Copy, **extra).then_inc(sem("xT"), 1)

            def take_h(it):
                act.wait_ge(sem("h_ps"), it.done)
                if it.l == LAYERS:
                    act.copy(split[:, it.r, 0, :, :], h_ps[:, :, 0:D]).then_inc(sem("split_hi"), 1)
                    return
                if it.l in (0, 2):
                    if not isinstance(it.g, int) or it.l > 0 or it.g >= 2:
                        act.wait_ge(sem("mean_raw"), halves(it) - 2)
                    act.activation(h_mean[:, it.b, :].rearrange("p (e d) -> p e d", e=2), h_mean_ps, ACT.Copy,
                                   scale=1.0 / N).then_inc(sem("h_mean"), 1)
                width = 131 if it.l == 0 else 130
                act.copy(hx[:, it.r, :, 1:1 + width], h_ps[:, :, 0:width]).then_inc(sem("hx"), 1)

            def node_factors(it):
                act.wait_ge(sem("shifts"), halves(it))
                for f, (s, scale) in enumerate(((S1, 1 - SLOPE), (S2, 1.0), (S2, SLOPE))):
                    last = act.activation(factors_raw[:, it.b, f, :], hx[:, it.r, :, s], ACT.Exp,
                                          scale=scale, bias=shifts[:, it.b, f:f + 1])
                last.then_inc(sem("factors_raw"), 1)

            def edges(it, cs):
                if cs[0] == 0:
                    act.wait_ge(sem("rows_ps"), it.done)
                    if it.l == 1:
                        if not isinstance(it.g, int) or it.g >= 1:
                            act.wait_ge(sem("edge_lin"), (it.of_layer - 1) * C)
                        act.copy(q_rows[:, 0, :], rows_ps[:])
                        act.activation(q_rows[:, 1, :], rows_ps[:], ACT.Copy, scale=SLOPE)\
                            .then_inc(sem("rows_taken"), 1)
                        act.wait_ge(sem("col_bias"), it.of_layer)
                    else:
                        act.wait_ge(sem("neg_d"), halves(it))
                for c in cs:
                    if it.l == 1:
                        act.wait_ge(sem("edge_lin"), (it.of_layer - 1) * C + (c + 1))
                        act.activation(edge[:, c, :], edge[:, c, :], ACT.Exp, bias=col_tmp[:, it.b, BIAS, c:c + 1],
                                       scale=col_tmp[:, it.b, FULL, c:c + 1]).then_inc(sem("edge"), 1)
                    else:
                        if not isinstance(it.g, int) or it.l > 0 or it.g >= 1:
                            act.wait_ge(sem("PT"), (it.done - 2) * C + (c + 1))
                        act.activation(edge[:, c, :], rows_ps[:], ACT.Relu, bias=neg_d[:, it.b, c:c + 1],
                                       scale=factors[:, it.b, 1, c:c + 1]).then_inc(sem("edge"), 1)

            def elu(it):
                if it.l == 1:
                    act.wait_ge(sem("att"), it.done)
                    src = o_ps[it.b][:, :, 1:1 + D]
                else:
                    act.wait_ge(sem("y_lin"), it.of_layer)
                    src = y[:, it.b, :, :]
                act.wait_ge(sem("y_sum"), it.done - 1)
                act.activation(elu_exp[:, :, :], src, ACT.Exp).then_inc(sem("elu_exp"), 1)

            def flag(it):
                act.wait_ge(sem(f"adj_in{it.r}"), landed(it))
                if not isinstance(it.g, int) or it.g >= 1:
                    act.wait_ge(sem("flag_sum"), it.of_layer - 1)
                act.activation(square_out[:, :], adj_in[:, it.b, :, :].rearrange("p c i -> p (c i)"), ACT.Square,
                               bias=minus_half[:, 0:1], accum_out=flag_sum[:, it.g, :])\
                    .then_inc(sem("flag_sum"), 1)

            def attention_slot(at, n):
                if at(-1) and at(-1).l == 1:
                    elu(at(-1))
                if at(1):
                    edges(at(1), (0, 1))
                if at(2):
                    take_h(at(2))
                if at(-1) and at(-1).l == 2:
                    elu(at(-1))
                if at(1):
                    edges(at(1), (2, 3))
                if at(3):
                    take_xT(at(3))
                if at(3) and at(3).l == 0:
                    flag(at(3))
                if at(2) and at(2).l in (0, 2):
                    node_factors(at(2))

            def relation_slot(at, n):
                if at(2):
                    take_h(at(2))
                if at(3):
                    take_xT(at(3))
                if at(2):
                    it = at(2)
                    act.wait_ge(sem("split_rest"), it.of_layer)
                    act.copy(split[:, it.r, 1, :, :], rest[:, :, :]).then_inc(sem("split_mid"), 1)

            pipeline(act, attention_slot, 0, LAYERS)
            with act.If(not_binary(act)):
                with act.Fori(0, G) as g:
                    act.wait_ge(sem("rel_xT_ps"), g + 1)
                    act.copy(xT[:, 0, :], xT_ps[:]).then_inc(sem("rel_xT"), 1)
                    for r in range(REL):
                        act.wait_ge(sem("rel_h_ps"), g * REL + (r + 1))
                        act.copy(split[:, 0, 0, :, :], h_ps[:, :, 0:D]).then_inc(sem("rel_split_hi"), 1)
                        act.wait_ge(sem("rel_split_rest"), g * REL + (r + 2))
                        act.copy(split[:, 0, 1, :, :], rest[:, :, :]).then_inc(sem("rel_split_mid"), 1)
            with act.Else():
                pipeline(act, relation_slot, G * LAYERS, 1)

        @block.vector
        def _(dve):
            dve.memset(minus_half[:], -0.5)
            dve.memset(ones_bf[:], 1.0).then_inc(sem("ready"), 1)
            dve.memset(shift_add[:], 0.0)
            for f, value in enumerate((1 - SLOPE, -1.0, -SLOPE)):
                dve.memset(shift_k[:, f:f + 1], value)
            dve.memset(hx[:, :, :, 0:1], 1.0).then_inc(sem("ones"), 1)
            dve.wait_ge(sem("wa"), 1)
            dve.tensor_tensor(b2_ab[:, :], b2_a[:, :], ab2_sb[:, :], ALU.add).then_inc(sem("b2_ab"), 1)
            dve.wait_ge(sem("b2_ab"), 1)
            dve.wait_ge(sem("ones"), 1)
            dve.tensor_scalar(shift_add[:, 2, 0:1], b2_ab[:, 0:1], b2_ab[:, 1:2], 1 - SLOPE, ALU.add,
                              ALU.mult).then_inc(sem("shift_add"), 1)
            dve.wait_ge(sem("shift_add"), 1)

            def mask(it):
                dve.wait_ge(sem(f"adj_in{it.r}"), landed(it))
                dve.tensor_scalar(MT[:, it.g, :, :], adj_in[:, it.b, :, :], 0, None, ALU.not_equal)\
                    .then_inc(sem("mask"), 1)

            def own_max(it):
                dve.wait_ge(sem("hx"), it.done)
                if it.l == 0:
                    dve.tensor_scalar(empty_row[:, it.g, :], hx[:, it.r, :, DEG], 0.0, None, ALU.is_equal)\
                        .then_inc(sem("empty_row"), 1)
                s = S1 if it.l == 1 else S2
                dve.tensor_reduce(smax_own[:, it.b:it.b + 1], hx[:, it.r, :, s], AX.X, ALU.max)\
                    .then_inc(sem("smax_own"), 1)

            def node_shifts(it):
                dve.wait_ge(sem("smax_ps"), it.done)
                dve.tensor_reduce(smax[:, it.b:it.b + 1], smax_ps, AX.XY, ALU.max).then_inc(sem("smax"), 1)
                dve.wait_ge(sem("smax"), it.done)
                if it.l in (0, 2):
                    dve.scalar_tensor_tensor(out=shifts[:, it.b, :], in0=shift_k[:, :],
                                             scalar=smax[:, it.b:it.b + 1], in1=shift_add[:, it.l, :],
                                             op0=ALU.mult, op1=ALU.add).then_inc(sem("shifts"), 1)
                    return
                r = hx[:, it.r, :, S2]
                t = col_tmp[:, it.b, :, :]
                dve.tensor_scalar(t[:, 0, :], r, smax[:, it.b:it.b + 1], -1.0, ALU.add, ALU.mult)\
                    .then_inc(sem("neg_z"), 1)
                dve.tensor_scalar(t[:, TILT, :], r, -(1 - SLOPE), None, ALU.mult).then_inc(sem("tilt"), 1)
                dve.wait_ge(sem("neg_z"), it.of_layer)
                dve.scalar_tensor_tensor(out=t[:, 1, :], in0=t[:, 0, :], scalar=SLOPE, in1=t[:, 0, :],
                                         op0=ALU.mult, op1=ALU.min).then_inc(sem("neg_m"), 1)
                dve.wait_ge(sem("neg_m"), it.of_layer)
                dve.tensor_tensor(t[:, 2, :], t[:, 1, :], r, ALU.add).then_inc(sem("r_minus_m"), 1)

            def node_factors(it):
                dve.wait_ge(sem("factors_raw"), halves(it))
                dve.tensor_scalar(factors[:, it.b, :, :], factors_raw[:, it.b, :, :], R_MAX, TINY, ALU.min,
                                  ALU.max).then_inc(sem("factors"), 1)
                dve.wait_ge(sem("factors"), halves(it))
                dve.tensor_scalar(neg_d[:, it.b, :], factors[:, it.b, 2, :], -1.0, None, ALU.mult)\
                    .then_inc(sem("neg_d"), 1)

            def column_terms(it):
                t = col_tmp[:, it.b, :, :]
                dve.tensor_scalar(t[:, FULL, :], empty_col[:, it.g, :], -1.0, 1.0, ALU.mult, ALU.add)\
                    .then_inc(sem("col_full"), 1)
                dve.wait_ge(sem("col_full"), it.of_layer)
                dve.wait_ge(sem("r_minus_m"), it.of_layer)
                dve.tensor_tensor(t[:, BIAS, :], t[:, 2, :], t[:, FULL, :], ALU.mult).then_inc(sem("col_bias"), 1)
                dve.wait_ge(sem("rows_taken"), it.of_layer)
                for c in range(C):
                    dve.scalar_tensor_tensor(out=edge[:, c, :], in0=q_rows[:, 1, :], scalar=t[:, TILT, c:c + 1],
                                             in1=q_rows[:, 0, :], op0=ALU.add, op1=ALU.max)\
                        .then_inc(sem("edge_lin"), 1)

            def weights(it, cs):
                if cs[0] == 0 and (not isinstance(it.g, int) or it.l > 0 or it.g >= 2):
                    dve.wait_ge(sem("att"), it.done - 2)
                for c in cs:
                    dve.wait_ge(sem("edge"), (it.done - 1) * C + (c + 1))
                    m = MT[:, it.g, c, :]
                    if it.l == 1:
                        dve.scalar_tensor_tensor(out=PT[:, it.b, c, :], in0=m, scalar=empty_col[:, it.g, c:c + 1],
                                                 in1=edge[:, c, :], op0=ALU.max, op1=ALU.mult,
                                                 accum_out=col_tmp[:, it.b, Z, c:c + 1]).then_inc(sem("PT"), 1)
                    else:
                        extra = dict(accum_out=col_sum[:, it.b, c:c + 1]) if it.l == 0 else {}
                        dve.scalar_tensor_tensor(out=PT[:, it.b, c, :], in0=edge[:, c, :],
                                                 scalar=factors[:, it.b, 2, c:c + 1], in1=m, op0=ALU.add,
                                                 op1=ALU.mult, **extra).then_inc(sem("PT"), 1)

            def column_sums(it):
                dve.wait_ge(sem("PT"), it.done * C)
                if it.l == 0:
                    dve.tensor_scalar(empty_col[:, it.g, :], col_sum[:, it.b, :], 0.0, None, ALU.is_equal)\
                        .then_inc(sem("empty_col"), 1)
                elif it.l == 1:
                    t = col_tmp[:, it.b, :, :]
                    dve.tensor_scalar(t[:, Z, :], t[:, Z, :], TINY, None, ALU.max).then_inc(sem("z_col"), 1)
                    dve.wait_ge(sem("z_col"), it.of_layer)
                    dve.reciprocal(t[:, RZ, :], t[:, Z, :]).then_inc(sem("rz_col"), 1)

            def take_out(it):
                o = o_ps[it.b]
                dve.wait_ge(sem("att"), it.done)
                if it.l in (0, 2):
                    dve.tensor_scalar(z_row[:, it.b, :], o[:, :, 0], TINY, None, ALU.max).then_inc(sem("z_row"), 1)
                    dve.wait_ge(sem("z_row"), halves(it))
                    dve.reciprocal(rz_row[:, it.b, :], z_row[:, it.b, :]).then_inc(sem("rz_row"), 1)
                    dve.wait_ge(sem("rz_row"), halves(it))
                    if it.l == 0:
                        dve.wait_ge(sem("residual"), it.done)
                    else:
                        dve.wait_ge(sem("mean_term"), it.of_layer)
                    add = residual if it.l == 0 else mean_term
                    for c in range(C):
                        last = dve.scalar_tensor_tensor(out=y[:, it.b, c, :], in0=o[:, c, 1:1 + D],
                                                        scalar=rz_row[:, it.b, c:c + 1], in1=add[:, it.b, c, :],
                                                        op0=ALU.mult, op1=ALU.add)
                    last.then_inc(sem("y_sum" if it.l == 0 else "y_lin"), 1)
                elif it.l == 1:
                    add_elu(it, o[:, :, 1:1 + D])
                else:
                    dve.wait_ge(sem("residual"), it.done)
                    dve.tensor_tensor(y[:, it.b, :, :], o[:, :, 1:1 + D], residual[:, it.b, :, :],
                                      ALU.add).then_inc(sem("y_sum"), 1)

            def add_elu(it, lin):
                dve.wait_ge(sem("elu_exp"), it.done - G)
                dve.wait_ge(sem("residual"), it.done)
                dve.scalar_tensor_tensor(out=elu_exp[:, :, :], in0=elu_exp[:, :, :], scalar=1.0,
                                         in1=residual[:, it.b, :, :], op0=ALU.min,
                                         op1=ALU.add).then_inc(sem("elu_low"), 1)
                dve.wait_ge(sem("elu_low"), it.done - G)
                dve.scalar_tensor_tensor(out=y[:, it.b, :, :], in0=lin, scalar=0.0, in1=elu_exp[:, :, :],
                                         op0=ALU.max, op1=ALU.add).then_inc(sem("y_sum"), 1)

            def moments(b, y_sem, stats_sem, done, name):
                dve.wait_ge(y_sem, done)
                for c in range(C):
                    last = dve.bn_stats(stats[:, c, :], y[:, b, c, :])
                last.then_inc(stats_sem, 1)
                settle(dve)
                dve.wait_ge(stats_sem, done)
                for c in range(C):
                    last = dve.bn_aggr(mean_var[:, b, c, :], stats[:, c, :])
                last.then_inc(sem(name), 1)

            def normalize(b, g, rstd_sem, done, name):
                dve.wait_ge(rstd_sem, done)
                for c in range(C):
                    last = dve.tensor_scalar(X[:, g, c, :], y[:, b, c, :], mean_var[:, b, c, 0:1],
                                             rstd[:, b, c:c + 1], ALU.subtract, ALU.mult)
                last.then_inc(sem(name), 1)

            def rebuild_masks():
                dve.wait_ge(sem("h_ps"), G)
                dve.wait_ge(sem("residual"), G)
                dve.sem_inc(sem("rebuild_taken"), 1)
                with dve.Fori(0, G) as g:
                    dve.wait_ge(sem("rebuild_in"), g * 32 + 32)
                    binary = square_out[:, :].rearrange("p (c i) -> p c i", c=C)
                    for side, empty in enumerate((empty_col, empty_row)):
                        if side:
                            dve.wait_ge(sem("rebuild_count"), g * 2 + 1)
                            dve.wait_ge(sem("rebuild_copied"), g + 1)
                        mark = dve.tensor_scalar(binary, adj_in[:, side, :, :], 0, None, ALU.is_gt)
                        mark.then_inc(sem("rebuild_taken" if side else "rebuild_mask"), 1)
                        if side:
                            dve.wait_ge(sem("rebuild_taken"), g + 2)
                        else:
                            dve.wait_ge(sem("rebuild_mask"), g + 1)
                            dve.tensor_copy(MT[:, g, :, :], binary).then_inc(sem("rebuild_copied"), 1)
                        dve.tensor_reduce(count[:, side, :], binary, AX.X, ALU.add).then_inc(sem("rebuild_count"), 1)
                        dve.wait_ge(sem("rebuild_count"), g * 2 + (side + 1))
                        dve.tensor_scalar(empty[:, g, :], count[:, side, :], 0.0, None, ALU.is_equal)\
                            .then_inc(sem("rebuild_done"), 1)
                dve.wait_ge(sem("rebuild_done"), 2 * G)

            def attention_slot(at, n):
                if n == G - 1:
                    with dve.If(not_binary(dve)):
                        rebuild_masks()
                if at(-1):
                    take_out(at(-1))
                if at(1) and at(1).l == 1:
                    column_terms(at(1))
                if at(3) and at(3).l == 0:
                    mask(at(3))
                if at(1):
                    weights(at(1), (0, 1))
                if at(2):
                    own_max(at(2))
                if at(-1) and at(-1).l == 2:
                    add_elu(at(-1), y[:, at(-1).b, :, :])
                if at(1):
                    weights(at(1), (2, 3))
                    column_sums(at(1))
                if at(2):
                    node_shifts(at(2))
                if at(-1):
                    moments(at(-1).b, sem("y_sum"), sem("stats"), at(-1).done, "mean_var")
                if at(2) and at(2).l in (0, 2):
                    node_factors(at(2))
                if at(-1):
                    normalize(at(-1).b, at(-1).g, sem("rstd"), at(-1).done, "x_new")
                if n == G - 3:
                    dve.wait_ge(sem("flag_sum"), G)
                    dve.tensor_reduce(flag_own[:, 0:1], flag_sum[:, :, 0], AX.X, ALU.max).then_inc(sem("flag_own"), 1)
                    dve.wait_ge(sem("flag_ps"), 1)
                    dve.tensor_reduce(flag_own[:, 1:2], xT_ps[:, 0:P], AX.X, ALU.max).then_inc(sem("flag_max"), 1)
                    dve.wait_ge(sem("flag_max"), 1)
                    dve.tensor_scalar(flag_int[:, :], flag_own[:, 1:2], 0.25 * C * N, None, ALU.is_gt)\
                        .then_inc(sem("flag"), 1)

            def relation_slot(at, n):
                if at(-1):
                    take_out(at(-1))
                if at(2):
                    it = at(2)
                    dve.wait_ge(sem("split_hi"), it.of_layer)
                    if not isinstance(it.g, int) or it.g >= 1:
                        dve.wait_ge(sem("split"), it.of_layer - 1)
                    dve.tensor_tensor(rest[:, :, :], h_ps[:, :, 0:D], split[:, it.r, 0, :, :], ALU.subtract)\
                        .then_inc(sem("split_rest"), 1)
                if at(-1):
                    moments(at(-1).b, sem("y_sum"), sem("stats"), at(-1).done, "mean_var")
                if at(2):
                    dve.wait_ge(sem("split_mid"), it.of_layer)
                    dve.tensor_tensor(split[:, it.r, 2, :, :], rest[:, :, :], split[:, it.r, 1, :, :], ALU.subtract)\
                        .then_inc(sem("split"), 1)
                if at(-1):
                    normalize(at(-1).b, at(-1).g, sem("rstd"), at(-1).done, "x_new")

            pipeline(dve, attention_slot, 0, LAYERS)
            with dve.If(not_binary(dve)):
                dve.sem_inc(sem("rel_adj_free"), 1)
                dve.sem_inc(sem("rel_x_new"), 1)
                dve.sem_inc(sem("rel_split_rest"), 1)
                with dve.Fori(0, G) as g:
                    dve.wait_ge(sem("rel_adj_in"), g * 16 + 16)
                    for r in range(REL):
                        n = g * REL + (r + 1)
                        last = dve.tensor_scalar(MT[:, g, :, :], adj_in[:, 0, :, :], r + 1, None, ALU.is_equal)
                        last.then_inc(sem("rel_mask"), 1)
                        dve.wait_ge(sem("rel_split_hi"), n)
                        dve.tensor_tensor(rest[:, :, :], h_ps[:, :, 0:D], split[:, 0, 0, :, :], ALU.subtract)\
                            .then_inc(sem("rel_split_rest"), 1)
                        dve.wait_ge(sem("rel_split_mid"), n)
                        dve.tensor_tensor(split[:, 0, 2, :, :], rest[:, :, :], split[:, 0, 1, :, :], ALU.subtract)\
                            .then_inc(sem("rel_split"), 1)
                        dve.wait_ge(sem("rel_att"), n)
                        if r == 0:
                            dve.wait_ge(sem("rel_residual"), g + 1)
                        else:
                            dve.wait_ge(sem("rel_sum"), g * (REL - 1) + r)
                        dve.tensor_tensor(y[:, 0, :, :], o_ps[0][:, :, 1:1 + D],
                                          residual[:, 0, :, :] if r == 0 else y[:, 0, :, :], ALU.add)\
                            .then_inc(sem("rel_total" if r == REL - 1 else "rel_sum"), 1)
                    dve.wait_ge(sem("rel_mask"), g * REL + REL)
                    dve.sem_inc(sem("rel_adj_free"), 1)
                    moments(0, sem("rel_total"), sem("rel_stats"), g + 1, "rel_mean_var")
                    normalize(0, g, sem("rel_rstd"), g + 1, "rel_x_new")
            with dve.Else():
                pipeline(dve, relation_slot, G * LAYERS, 1)


def kernel(x, adj, L0_gnn_W, L0_gnn_a, L1_gnn_W, L1_gnn_a, L2_gnn_W_w, L2_gnn_W_b, L2_gnn_ai_w, L2_gnn_ai_b,
           L2_gnn_aj_w, L2_gnn_aj_b, L3_gnn_adj, L3_gnn_weight, L3_gnn_bias):
    import numpy as np
    import concourse.bacc as bacc
    from concourse.bass_utils import run_bass_kernel_spmd

    x, adj = np.asarray(x), np.asarray(adj)
    w0, w1, w2 = (np.asarray(w) for w in (L0_gnn_W, L1_gnn_W, L2_gnn_W_w))
    arrays = {
        "x": x.reshape(G, C, P, D).transpose(0, 2, 1, 3),
        "adj_by_j": adj.transpose(0, 2, 1).reshape(G, C, P, N).transpose(0, 2, 1, 3),
        "adj_by_i": adj.reshape(G, C, P, N).transpose(0, 2, 1, 3),
        "w0": w0, "w0t": w0.T, "a0": np.asarray(L0_gnn_a).reshape(2, D).T,
        "w1": w1, "w1t": w1.T, "a1": np.asarray(L1_gnn_a).reshape(2, D).T,
        "w2": w2, "w2t": w2.T,
        "a2": np.concatenate([np.asarray(L2_gnn_ai_w), np.asarray(L2_gnn_aj_w)]).T,
        "b2": np.asarray(L2_gnn_W_b),
        "ab2": np.concatenate([np.asarray(L2_gnn_ai_b), np.asarray(L2_gnn_aj_b)]),
        "w3": np.asarray(L3_gnn_weight), "b3": np.asarray(L3_gnn_bias),
    }
    arrays = {name: np.ascontiguousarray(a) for name, a in arrays.items()}
    nc = bacc.Bacc("TRN2", target_bir_lowering=False, num_devices=1)
    args = [nc.dram_tensor(name, a.shape, mybir.dt.from_np(a.dtype), kind="ExternalInput").ap()
            for name, a in arrays.items()]
    out = nc.dram_tensor("out", (G, P, C, D), F32, kind="ExternalOutput").ap()
    build(nc, *args, out)
    got = run_bass_kernel_spmd(nc, [arrays], core_ids=[0])
    return np.asarray(got.results[0]["out"]).reshape(G, P, C, D).transpose(0, 2, 1, 3).reshape(G, N, D)
```

```python
from contextlib import ExitStack

import concourse.bass as bass
from concourse import mybir

F32 = mybir.dt.float32
BF16 = mybir.dt.bfloat16
I32 = mybir.dt.int32
ALU = mybir.AluOpType
ACT = mybir.ActivationFunctionType
AX = mybir.AxisListType

P = 128
G = 16
N = 512
D = 128
C = N // P
REL = 4
EPS = 1e-5
SLOPE = 0.2
R_MAX = 5.5e34
TINY = 1e-37
LAYERS = 3
NORM_ON_POOL = (0,)
UNROLL = 4
S1, S2, DEG = 129, 130, 131
LOOP_START, LOOP_END = 4, 12
R_EIGHTY, EXPONENT, BIAS, Z, RZ = range(5)


class Item:

    def __init__(self, l, g, r):
        self.l, self.g, self.r, self.b = l, g, r % 4, r % 2
        self.done = g + (G * l + 1)
        self.of_layer = g + 1


def item(n):
    return Item(n // G, n % G, n % G) if n >= 0 else None


def build(nc, x, adj, adj_rows, w0, w0t, a0, w1, w1t, a1, w2, w2t, a2, b2, ab2, w3, b3, out):
    ctx = ExitStack()
    with ctx:
        def sb(name, shape, dt=F32):
            return ctx.enter_context(nc.sbuf_tensor(name, shape, dt))

        def pb(name, shape, dt=F32):
            return ctx.enter_context(nc.psum_tensor(name, shape, dt))

        sems = {}

        def sem(name):
            if name not in sems:
                sems[name] = ctx.enter_context(nc.semaphore(name))
            return sems[name]

        X = sb("X", [P, G, C, D])
        MT = sb("MT", [P, G, C, N], BF16)
        adj_in = sb("adj_in", [P, 2, C, N], I32)
        square_out = sb("square_out", [P, C * N], BF16)
        flag_sum = sb("flag_sum", [P, G, 1])
        empty_row = sb("empty_row", [P, G, C])
        empty_col = sb("empty_col", [P, G, C])
        x_cur = sb("x_cur", [P, 2, C, D])
        xT = sb("xT", [P, 2, N])
        x_sum = sb("x_sum", [P, 2])
        hx = sb("hx", [P, 4, C, 132])
        h_mean = sb("h_mean", [P, 2, D])
        h_scaled = sb("h_scaled", [P, 2, C, D])
        smax_own = sb("smax_own", [P, 2])
        smax = sb("smax", [P, 2])
        shifts = sb("shifts", [P, 2, 3])
        factors_raw = sb("factors_raw", [P, 2, 3, C])
        factors = sb("factors", [P, 2, 3, C])
        neg_d = sb("neg_d", [P, 2, C])
        q_rows = sb("q_rows", [P, 2, N])
        edge = sb("edge", [P, C, N])
        PT = sb("PT", [P, 2, C, N])
        col_tmp = sb("col_tmp", [P, 2, 5, C])
        col_full = sb("col_full", [P, G, C])
        residual = sb("residual", [P, 2, C, D])
        mean_term = sb("mean_term", [P, 2, C, D])
        z_row = sb("z_row", [P, 2, C])
        rz_row = sb("rz_row", [P, 2, C])
        y = sb("y", [P, 2, C, D])
        elu_exp = sb("elu_exp", [P, C, D])
        stats = sb("stats", [P, C, 6])
        mean_var = sb("mean_var", [P, 2, C, 2])
        var_eps = sb("var_eps", [P, 2, C])
        rstd = sb("rstd", [P, 2, C])
        neg_mean = sb("neg_mean", [P, 2, C])
        offset = sb("offset", [P, 2, C])
        elu_low_arg = sb("elu_low_arg", [P, C, D])
        centered = sb("centered", [P, C, D])
        split = sb("split", [P, 4, 3, C, D], BF16)
        rest = sb("rest", [P, C, D])
        elu_high = rest
        ident = sb("ident", [P, P])
        ones_bf = sb("ones_bf", [P, 1], BF16)
        col_sum = sb("col_sum", [P, 2, C])
        count = sb("count", [P, 2, C])
        flag_own = sb("flag_own", [P, 2])
        neg_half = sb("neg_half", [P, C])
        eps_tile = sb("eps_tile", [P, C])
        minus_one = sb("minus_one", [P, C])
        minus_half = sb("minus_half", [P, 1])
        wx = sb("wx", [P, 3, 130])
        w_back = sb("w_back", [P, 3, D])
        a_cols = sb("a_cols", [P, 3, 2])
        w_rel = sb("w_rel", [P, REL, D])
        bias2 = sb("bias2", [P, D])
        bias2_col = sb("bias2_col", [P, 1])
        bias3 = sb("bias3", [P, D])
        ab2_sb = sb("ab2_sb", [P, 2])
        shift_k = sb("shift_k", [P, 5])
        b2_a = sb("b2_a", [P, 2])
        b2_ab = sb("b2_ab", [P, 2])
        shift_add = sb("shift_add", [P, LAYERS, 3])
        flag_int = sb("flag_int", [P, 1], I32)

        xT_ps = pb("xT_ps", [P, N])
        h_ps = pb("h_ps", [P, C, 256])
        rows_ps = pb("rows_ps", [P, N])
        o_ps = [pb(f"o_ps{b}", [P, C, 256]) for b in range(2)]
        h_mean_ps = h_ps[:, 2:4, 132:196]
        smax_ps = h_ps[:, 0:2, 132:196]

        block = ctx.enter_context(nc.Block())

        def pipeline(eng, slot, first, layers):
            last = first + G * layers
            n = first - 4
            while n <= last + 1:
                if n >= first and n % G == LOOP_START:
                    l = n // G
                    with eng.Fori(LOOP_START, LOOP_END - UNROLL + 1, UNROLL) as i:
                        for u in range(UNROLL):
                            slot(lambda k, u=u: Item(l, i + (u + k), u + k + 4), None)
                    n += LOOP_END - LOOP_START
                else:
                    slot(lambda k, n=n: item(n + k) if first <= n + k < last else None, n)
                    n += 1

        def halves(it):
            return it.of_layer + (G if it.l == 2 else 0)

        def landed(it):
            return 16 * (it.g // 4 + 1) if isinstance(it.g, int) else it.g * 4 + (16 - 4 * it.r)

        def settle(eng):
            eng.wait_ge(sem("ready"), 1)

        def not_binary(eng):
            eng.wait_ge(sem("flag"), 1)
            return eng.value_load(flag_int[0:1, 0:1], min_val=0, max_val=1) > 0

        @block.sync
        def _(sp):

            def load(it):
                settle(sp)
                if not isinstance(it.g, int) or it.g >= 2:
                    sp.wait_ge(sem("mask"), it.of_layer - 2)
                    sp.wait_ge(sem("flag_sum"), it.of_layer - 2)
                sp.dma_start(adj_in[:, it.b, :, :], adj[it.g, :, :, :]).then_inc(sem(f"adj_in{it.r}"), 16)

            def load_x(n):
                sp.dma_start(X[:, 4 * n:4 * n + 4, :, :], x[4 * n:4 * n + 4, :, :, :].rearrange("g p c d -> p g c d"))\
                    .then_inc(sem(f"x_in{n}"), 16)

            def copy_x(it):
                if it.l == 0:
                    for quarter in range(4) if not isinstance(it.g, int) else (0,):
                        sp.wait_ge(sem(f"x_in{quarter}"), 16)
                settle(sp)
                if not isinstance(it.g, int) or it.l > 0 or it.g >= 2:
                    sp.wait_ge(sem("xT_ps"), it.done - 2)
                sp.dma_start(x_cur[:, it.b, :, :], X[:, it.g, :, :]).then_inc(sem(f"x_cur{it.r}"), 16)

            def copy_layer(l):
                with sp.Fori(0, G - UNROLL + 1, UNROLL) as i:
                    for u in range(UNROLL):
                        copy_x(Item(l, i + u, u))

            load_x(0)
            load(item(0))
            load(item(1))
            copy_x(item(0))
            copy_x(item(1))
            for n in (2, 3):
                load(item(n))
                copy_x(item(n))
                load_x(n - 1)
            load_x(3)
            sp.dma_start(w_rel[:, :, :], w3.rearrange("r d o -> d r o")).then_inc(sem("w_late"), 16)
            sp.dma_start(bias3[:, :], b3.partition_broadcast(P)).then_inc(sem("w_late"), 16)
            with sp.Fori(4, G - UNROLL + 1, UNROLL) as i:
                for u in range(UNROLL):
                    load(Item(0, i + u, u))
                    copy_x(Item(0, i + u, u))
            for n in range(G, G + 3):
                copy_x(item(n))
            with sp.If(not_binary(sp)):
                with sp.Fori(0, G) as g:
                    settle(sp)
                    sp.wait_ge(sem("rebuild_taken"), g + 1)
                    sp.dma_start(adj_in[:, 0, :, :], adj[g, :, :, :]).then_inc(sem("rebuild_in"), 16)
                    sp.dma_start(adj_in[:, 1, :, :], adj_rows[g, :, :, :]).then_inc(sem("rebuild_in"), 16)
            copy_x(item(G + 3))
            with sp.Fori(4, G - UNROLL + 1, UNROLL) as i:
                for u in range(UNROLL):
                    copy_x(Item(1, i + u, u))
            copy_layer(2)

            with sp.If(not_binary(sp)):
                with sp.Fori(0, G) as g:
                    settle(sp)
                    sp.wait_ge(sem("rel_adj_free"), g + 1)
                    sp.dma_start(adj_in[:, 0, :, :], adj[g, :, :, :]).then_inc(sem("rel_adj_in"), 16)
                with sp.Fori(0, G) as g:
                    settle(sp)
                    sp.wait_ge(sem("rel_x_new"), g + 2)
                    sp.dma_start(out[g, :, :, :], X[:, g, :, :]).then_inc(sem("rel_out"), 16)
                sp.wait_ge(sem("rel_out"), 16 * G)
            with sp.Else():
                copy_layer(LAYERS)

        W_IN = 16 * 12

        @block.gpsimd
        def _(pool):
            pool.memset(ident[:], 0.0).then_inc(sem("ident_zero"), 1)
            pool.wait_ge(sem("ident_zero"), 1)
            pool.affine_select(out=ident[:], in_=ident[:], compare_op=ALU.not_equal, fill=1.0, base=0,
                               pattern=[[-1, P]], channel_multiplier=1).then_inc(sem("ident"), 1)
            pool.memset(neg_half[:], -0.5)
            pool.memset(eps_tile[:], EPS)
            pool.memset(minus_one[:], -1.0).then_inc(sem("pool_const"), 1)
            pool.wait_ge(sem("pool_const"), 1)

            def mean(it):
                settle(pool)
                if it.l == 2:
                    if not isinstance(it.g, int) or it.g >= 2:
                        pool.wait_ge(sem("y_lin"), it.of_layer - 2)
                elif not isinstance(it.g, int) or it.g >= 2:
                    pool.wait_ge(sem("residual"), it.done - 2)
                pool.wait_ge(sem("h_mean"), halves(it))
                if it.l == 0:
                    pool.wait_ge(sem("empty_row"), it.of_layer)
                pool.tensor_tensor(mean_term[:, it.b, :, :],
                                   h_mean[:, it.b, :].unsqueeze(1).broadcast_to([P, C, D]),
                                   empty_row[:, it.g, :].unsqueeze(2).broadcast_to([P, C, D]),
                                   ALU.mult).then_inc(sem("mean_raw"), 1)
                if it.l == 2:
                    settle(pool)
                    pool.wait_ge(sem("mean_raw"), halves(it))
                    pool.tensor_tensor(mean_term[:, it.b, :, :], mean_term[:, it.b, :, :],
                                       bias2[:, :].unsqueeze(1).broadcast_to([P, C, D]),
                                       ALU.add).then_inc(sem("mean_term"), 1)

            def add_residual(it):
                xg = X[:, it.g, :, :]
                settle(pool)
                if it.l == 2:
                    pool.wait_ge(sem("elu_low"), it.done - (G + 2))
                elif not isinstance(it.g, int) or it.l > 0 or it.g >= 2:
                    pool.wait_ge(sem("y_sum"), it.done - 2)
                if it.l == 0:
                    pool.wait_ge(sem("mean_raw"), it.done)
                    pool.tensor_tensor(residual[:, it.b, :, :], xg, mean_term[:, it.b, :, :],
                                       ALU.add).then_inc(sem("residual"), 1)
                    return
                pool.tensor_tensor(residual[:, it.b, :, :], xg, minus_one[:, :].unsqueeze(2).broadcast_to([P, C, D]),
                                   ALU.add).then_inc(sem("residual"), 1)

            def scale_h(it):
                pool.wait_ge(sem("rz_col"), it.of_layer)
                pool.wait_ge(sem("att"), it.done - 2)
                pool.tensor_tensor(h_scaled[:, it.b, :, :], hx[:, it.r, :, 1:1 + D],
                                   col_tmp[:, it.b, RZ, :].unsqueeze(2).broadcast_to([P, C, D]),
                                   ALU.mult).then_inc(sem("h_scaled"), 1)

            def rsqrt(b, mean_var_sem, names, done):
                pool.wait_ge(mean_var_sem, done)
                pool.tensor_tensor(var_eps[:, b, :], mean_var[:, b, :, 1], eps_tile[:], ALU.add)\
                    .then_inc(sem(names[0]), 1)
                pool.wait_ge(sem(names[0]), done)
                pool.tensor_tensor(rstd[:, b, :], var_eps[:, b, :], neg_half[:], ALU.pow)\
                    .then_inc(sem(names[1]), 1)
                pool.wait_ge(sem(names[1]), done)
                pool.tensor_tensor(offset[:, b, :], neg_mean[:, b, :], rstd[:, b, :], ALU.mult)\
                    .then_inc(sem(names[2]), 1)

            def normalize(it):
                if not isinstance(it.g, int) or it.l > 0 or it.g >= 1:
                    pool.wait_ge(sem("x_new"), it.done - 1)
                pool.tensor_tensor(centered[:, :, :], y[:, it.b, :, :],
                                   mean_var[:, it.b, :, 0].unsqueeze(2).broadcast_to([P, C, D]),
                                   ALU.subtract).then_inc(sem("centered"), 1)
                settle(pool)
                pool.wait_ge(sem("centered"), it.done)
                pool.tensor_tensor(X[:, it.g, :, :], centered[:, :, :],
                                   rstd[:, it.b, :].unsqueeze(2).broadcast_to([P, C, D]),
                                   ALU.mult).then_inc(sem("x_new"), 1)

            def elu_low(it):
                pool.wait_ge(sem("elu_exp"), it.done - G)
                pool.wait_ge(sem("residual"), it.done)
                pool.tensor_tensor(elu_exp[:, :, :], elu_exp[:, :, :], residual[:, it.b, :, :], ALU.add)\
                    .then_inc(sem("elu_low"), 1)
                if it.l == 1:
                    pool.wait_ge(sem("elu_low"), it.done - G)
                    pool.wait_ge(sem("elu_high"), it.of_layer)
                    pool.wait_ge(sem("x_new"), it.done - 2)
                    pool.tensor_tensor(y[:, it.b, :, :], elu_high[:, :, :], elu_exp[:, :, :], ALU.add)\
                        .then_inc(sem("y_sum"), 1)

            def attention_slot(at, n):
                if at(-1) and at(-1).l == 1:
                    elu_low(at(-1))
                if at(1) and at(1).l != 1:
                    mean(at(1))
                if at(-2) and at(-2).l == 2:
                    rsqrt(at(-2).b, sem("mean_var"), ("var_eps", "rstd", "offset"), at(-2).done)
                if at(-1) and at(-1).l == 2:
                    elu_low(at(-1))
                if at(-2) and at(-2).l in NORM_ON_POOL:
                    normalize(at(-2))
                if at(-1) and at(-1).l != 2:
                    rsqrt(at(-1).b, sem("mean_var"), ("var_eps", "rstd", "offset"), at(-1).done)
                if at(1):
                    add_residual(at(1))
                if at(1) and at(1).l == 1:
                    scale_h(at(1))

            def relation_slot(at, n):
                if at(1):
                    it = at(1)
                    settle(pool)
                    pool.wait_ge(sem("y_sum"), it.done - 2)
                    pool.tensor_tensor(residual[:, it.b, :, :], X[:, it.g, :, :],
                                       bias3[:, :].unsqueeze(1).broadcast_to([P, C, D]),
                                       ALU.add).then_inc(sem("residual"), 1)
                if at(-1):
                    rsqrt(at(-1).b, sem("mean_var"), ("var_eps", "rstd", "offset"), at(-1).done)

            pipeline(pool, attention_slot, 0, LAYERS)
            pool.wait_ge(sem("w_late"), 32)
            with pool.If(not_binary(pool)):
                with pool.Fori(0, G) as g:
                    pool.wait_ge(sem("x_new"), g + (G * 2 + 1))
                    pool.wait_ge(sem("rel_x_new"), g + 1)
                    pool.tensor_copy(x_cur[:, 0, :, :], X[:, g, :, :]).then_inc(sem("rel_x_cur"), 1)
                    pool.tensor_tensor(residual[:, 0, :, :], X[:, g, :, :],
                                       bias3[:, :].unsqueeze(1).broadcast_to([P, C, D]),
                                       ALU.add).then_inc(sem("rel_residual"), 1)
                    rsqrt(0, sem("rel_mean_var"), ("rel_var_eps", "rel_rstd", "rel_offset"), g + 1)
            with pool.Else():
                pipeline(pool, relation_slot, G * LAYERS, 1)

        @block.tensor
        def _(pe):
            pe.wait_ge(sem("w_in"), W_IN)
            for l in range(LAYERS):
                pe.matmul(xT_ps[:, 2 * l:2 * l + 2], w_back[:, l, :], a_cols[:, l, :], start=True, stop=True)
            pe.matmul(xT_ps[:, 6:8], bias2_col[:, 0:1].broadcast_to([P, P]), a_cols[:, 2, :],
                      start=True, stop=True).then_inc(sem("wa_ps"), 1)
            pe.wait_ge(sem("ident"), 1)
            pe.wait_ge(sem("wa"), 1)
            pe.wait_ge(sem("ones"), 1)

            def transpose_x(x_sem, done, b):
                pe.wait_ge(x_sem, done)
                for c in range(C):
                    last = pe.transpose(xT_ps[:, c * P:(c + 1) * P], x_cur[:, b, c, :], ident[:])
                return last

            def next_transpose(it):
                if not isinstance(it.g, int) or it.l > 0 or it.g >= 1:
                    pe.wait_ge(sem("xT"), it.done - 1)
                transpose_x(sem(f"x_cur{it.r}"), landed(it) + 4 * G * it.l, it.b).then_inc(sem("xT_ps"), 1)

            def project(it):
                pe.wait_ge(sem("xT"), it.done)
                if it.l < LAYERS:
                    if not isinstance(it.g, int) or it.l > 0 or it.g >= 1:
                        pe.wait_ge(sem("hx"), it.done - 1)
                        pe.wait_ge(sem("smax"), it.done - 1)
                elif not isinstance(it.g, int) or it.g >= 1:
                    pe.wait_ge(sem("split_rest"), it.of_layer - 1)
                if it.l == 0:
                    pe.wait_ge(sem("mask"), it.of_layer)
                for c in range(C):
                    lhsT = xT[:, it.b, c * P:(c + 1) * P]
                    if it.l < LAYERS:
                        last = pe.matmul(h_ps[:, c, 0:130], lhsT, wx[:, it.l, :], start=True, stop=True)
                    else:
                        last = pe.matmul(h_ps[:, c, 0:D], lhsT, w_rel[:, 0, :], start=True, stop=True)
                if it.l in (0, 2):
                    for e in range(2):
                        last = pe.matmul(h_mean_ps[:, e, :], x_sum[:, it.b:it.b + 1].broadcast_to([P, P]),
                                         wx[:, it.l, e * 64:(e + 1) * 64], start=True, stop=True)
                if it.l == 0:
                    for ic in range(C):
                        for jc in range(C):
                            last = pe.matmul(h_ps[:, ic, 130:131], MT[:, it.g, jc, ic * P:(ic + 1) * P],
                                             ones_bf[:, 0:1], start=(jc == 0), stop=(jc == C - 1))
                last.then_inc(sem("h_ps"), 1)

            def spread_max(it):
                pe.wait_ge(sem("smax_own"), it.done)
                pe.transpose(smax_ps, smax_own[:, it.b:it.b + 1].broadcast_to([P, P]), ident[:])\
                    .then_inc(sem("smax_ps"), 1)

            def spread_rows(it):
                if it.l == 1:
                    pe.wait_ge(sem("hx"), it.done)
                else:
                    pe.wait_ge(sem("factors"), halves(it))
                if not isinstance(it.g, int) or it.l > 0 or it.g >= 1:
                    pe.wait_ge(sem("edge"), (it.done - 1) * C)
                for c in range(C):
                    col = hx[:, it.r, c, S1:S1 + 1] if it.l == 1 else factors[:, it.b, 0, c:c + 1]
                    last = pe.transpose(rows_ps[:, c * P:(c + 1) * P], col.broadcast_to([P, P]), ident[:])
                last.then_inc(sem("rows_ps"), 1)

            def attend(it):
                pe.wait_ge(sem("PT"), it.done * C)
                if it.l == 1:
                    pe.wait_ge(sem("h_scaled"), it.of_layer)
                for ic in range(C):
                    for jc in range(C):
                        lhsT = PT[:, it.b, jc, ic * P:(ic + 1) * P]
                        if it.l == 1:
                            last = pe.matmul(o_ps[it.b][:, ic, 1:1 + D], lhsT, h_scaled[:, it.b, jc, :],
                                             start=(jc == 0), stop=(jc == C - 1))
                        else:
                            last = pe.matmul(o_ps[it.b][:, ic, 0:1 + D], lhsT, hx[:, it.r, jc, 0:1 + D],
                                             start=(jc == 0), stop=(jc == C - 1))
                last.then_inc(sem("att"), 1)

            def attention_slot(at, n):
                if at(1):
                    spread_rows(at(1))
                if at(2):
                    spread_max(at(2))
                if n == G - 2:
                    pe.wait_ge(sem("flag_own"), 1)
                    pe.wait_ge(sem("xT"), at(3).done)
                    pe.transpose(xT_ps[:, 0:P], flag_own[:, 0:1].broadcast_to([P, P]), ident[:])\
                        .then_inc(sem("flag_ps"), 1)
                    pe.wait_ge(sem("flag_max"), 1)
                if at(4):
                    next_transpose(at(4))
                if at(3):
                    project(at(3))
                if at(0):
                    attend(at(0))

            def relate(o, g, r, first, final):
                for ic in range(C):
                    for jc in range(C):
                        for part in range(3):
                            last = pe.matmul(o[:, ic, 1:1 + D], MT[:, g, jc, ic * P:(ic + 1) * P],
                                             split[:, r, part, jc, :], start=(first and jc == 0 and part == 0),
                                             stop=(final and jc == C - 1 and part == 2),
                                             skip_group_check=not (first and final))
                return last

            def relation_slot(at, n):
                if at(4):
                    next_transpose(at(4))
                if at(3):
                    project(at(3))
                if at(0):
                    it = at(0)
                    pe.wait_ge(sem("split"), it.of_layer)
                    pe.wait_ge(sem("y_sum"), it.done - 2)
                    relate(o_ps[it.b], it.g, it.r, True, True).then_inc(sem("att"), 1)

            pipeline(pe, attention_slot, 0, LAYERS)
            pe.wait_ge(sem("w_late"), 32)
            pe.wait_ge(sem("y_sum"), G * LAYERS)
            with pe.If(not_binary(pe)):
                with pe.Fori(0, G) as g:
                    transpose_x(sem("rel_x_cur"), g + 1, 0).then_inc(sem("rel_xT_ps"), 1)
                    pe.wait_ge(sem("rel_xT"), g + 1)
                    for r in range(REL):
                        pe.wait_ge(sem("rel_split_rest"), g * REL + (r + 1))
                        for c in range(C):
                            last = pe.matmul(h_ps[:, c, 0:D], xT[:, 0, c * P:(c + 1) * P], w_rel[:, r, :],
                                             start=True, stop=True)
                        last.then_inc(sem("rel_h_ps"), 1)
                        pe.wait_ge(sem("rel_split"), g * REL + (r + 1))
                        pe.wait_ge(sem("rel_mask"), g * REL + (r + 1))
                        relate(o_ps[0], g, 0, True, True).then_inc(sem("rel_att"), 1)
            with pe.Else():
                pipeline(pe, relation_slot, G * LAYERS, 1)

        @block.scalar
        def _(act):
            for l, (w, wb, a) in enumerate(((w0t, w0, a0), (w1, w1t, a1), (w2t, w2, a2))):
                act.dma_start(wx[:, l, 0:D], w).then_inc(sem("w_in"), 16)
                act.dma_start(w_back[:, l, :], wb).then_inc(sem("w_in"), 16)
                act.dma_start(a_cols[:, l, :], a).then_inc(sem("w_in"), 16)
            act.dma_start(bias2_col[:, :], b2.rearrange("(p o) -> p o", o=1)).then_inc(sem("w_in"), 16)
            act.dma_start(bias2[:, :], b2.partition_broadcast(P)).then_inc(sem("w_in"), 16)
            act.dma_start(ab2_sb[:, :], ab2.partition_broadcast(P)).then_inc(sem("w_in"), 16)
            act.wait_ge(sem("wa_ps"), 1)
            for l in range(LAYERS):
                act.copy(wx[:, l, D:D + 2], xT_ps[:, 2 * l:2 * l + 2])
            act.copy(b2_a[:, :], xT_ps[:, 6:8]).then_inc(sem("wa"), 1)
            act.wait_ge(sem("ones"), 1)

            def take_xT(it):
                act.wait_ge(sem("xT_ps"), it.done)
                if not isinstance(it.g, int) or it.l > 0 or it.g >= 2:
                    act.wait_ge(sem("h_ps"), it.done - 2)
                extra = dict(accum_out=x_sum[:, it.b:it.b + 1]) if it.l in (0, 2) else {}
                act.activation(xT[:, it.b, :], xT_ps[:], ACT.Copy, **extra).then_inc(sem("xT"), 1)

            def take_h(it):
                act.wait_ge(sem("h_ps"), it.done)
                if it.l == LAYERS:
                    act.copy(split[:, it.r, 0, :, :], h_ps[:, :, 0:D]).then_inc(sem("split_hi"), 1)
                    return
                if it.l in (0, 2):
                    if not isinstance(it.g, int) or it.l > 0 or it.g >= 2:
                        act.wait_ge(sem("mean_raw"), halves(it) - 2)
                    act.activation(h_mean[:, it.b, :].rearrange("p (e d) -> p e d", e=2), h_mean_ps, ACT.Copy,
                                   scale=1.0 / N).then_inc(sem("h_mean"), 1)
                width = 131 if it.l == 0 else 130
                act.copy(hx[:, it.r, :, 1:1 + width], h_ps[:, :, 0:width]).then_inc(sem("hx"), 1)

            def node_factors(it):
                act.wait_ge(sem("shifts"), halves(it))
                for f, (s, scale) in enumerate(((S1, 1 - SLOPE), (S2, 1.0), (S2, SLOPE))):
                    last = act.activation(factors_raw[:, it.b, f, :], hx[:, it.r, :, s], ACT.Exp,
                                          scale=scale, bias=shifts[:, it.b, f:f + 1])
                last.then_inc(sem("factors_raw"), 1)

            def take_rows(it):
                act.wait_ge(sem("rows_ps"), it.done)
                if not isinstance(it.g, int) or it.g >= 1:
                    act.wait_ge(sem("edge_lin"), (it.of_layer - 1) * C)
                act.copy(q_rows[:, 0, :], rows_ps[:])
                act.activation(q_rows[:, 1, :], rows_ps[:], ACT.Copy, scale=SLOPE).then_inc(sem("rows_taken"), 1)

            def edges(it, cs):
                if cs[0] == 0:
                    if it.l == 1:
                        act.wait_ge(sem("col_bias"), it.of_layer)
                    else:
                        act.wait_ge(sem("rows_ps"), it.done)
                        act.wait_ge(sem("neg_d"), halves(it))
                for c in cs:
                    if it.l == 1:
                        act.wait_ge(sem("edge_lin"), (it.of_layer - 1) * C + (c + 1))
                        act.activation(edge[:, c, :], edge[:, c, :], ACT.Exp, bias=col_tmp[:, it.b, BIAS, c:c + 1],
                                       scale=col_full[:, it.g, c:c + 1]).then_inc(sem("edge"), 1)
                    else:
                        if not isinstance(it.g, int) or it.l > 0 or it.g >= 1:
                            act.wait_ge(sem("PT"), (it.done - 2) * C + (c + 1))
                        act.activation(edge[:, c, :], rows_ps[:], ACT.Relu, bias=neg_d[:, it.b, c:c + 1],
                                       scale=factors[:, it.b, 1, c:c + 1]).then_inc(sem("edge"), 1)

            def elu(it):
                if it.l == 1:
                    act.wait_ge(sem("att"), it.done)
                    src = o_ps[it.b][:, :, 1:1 + D]
                else:
                    act.wait_ge(sem("y_lin"), it.of_layer)
                    src = y[:, it.b, :, :]
                if it.l == 1:
                    act.wait_ge(sem("y_sum"), it.done - 1)
                    act.activation(elu_high[:, :, :], src, ACT.Relu).then_inc(sem("elu_high"), 1)
                if not isinstance(it.g, int) or it.l > 1 or it.g >= 1:
                    act.wait_ge(sem("elu_exp"), it.done - (G + 1))
                act.activation(elu_low_arg[:, :, :], src, ACT.Relu, scale=-1.0).then_inc(sem("elu_low_arg"), 1)
                act.wait_ge(sem("elu_low_arg"), it.done - G)
                if it.l == 2:
                    act.wait_ge(sem("y_sum"), it.done - 1)
                act.activation(elu_exp[:, :, :], elu_low_arg[:, :, :], ACT.Exp, scale=-1.0)\
                    .then_inc(sem("elu_exp"), 1)

            def normalize(b, g, offset_sem, done, name):
                act.wait_ge(offset_sem, done)
                for c in range(C):
                    last = act.activation(X[:, g, c, :], y[:, b, c, :], ACT.Identity, bias=offset[:, b, c:c + 1],
                                          scale=rstd[:, b, c:c + 1])
                last.then_inc(sem(name), 1)

            def flag(it):
                act.wait_ge(sem(f"adj_in{it.r}"), landed(it))
                if not isinstance(it.g, int) or it.g >= 1:
                    act.wait_ge(sem("flag_sum"), it.of_layer - 1)
                act.activation(square_out[:, :], adj_in[:, it.b, :, :].rearrange("p c i -> p (c i)"), ACT.Square,
                               bias=minus_half[:, 0:1], accum_out=flag_sum[:, it.g, :])\
                    .then_inc(sem("flag_sum"), 1)

            def attention_slot(at, n):
                if at(1) and at(1).l == 1:
                    take_rows(at(1))
                if at(-1) and at(-1).l == 1:
                    elu(at(-1))
                if at(1):
                    edges(at(1), (0, 1))
                if at(2) and at(2).l in (0, 2):
                    node_factors(at(2))
                if at(1):
                    edges(at(1), (2, 3))
                if at(4):
                    take_xT(at(4))
                if at(-1) and at(-1).l == 2:
                    elu(at(-1))
                if at(3):
                    take_h(at(3))
                if at(-2) and at(-2).l not in NORM_ON_POOL:
                    if n == G + 2:
                        act.wait_ge(sem("x_new"), G)
                    normalize(at(-2).b, at(-2).g, sem("offset"), at(-2).done, "x_new")
                if at(4) and at(4).l == 0:
                    flag(at(4))

            def relation_slot(at, n):
                if at(4):
                    take_xT(at(4))
                if at(3):
                    take_h(at(3))
                if at(-2):
                    it = at(-2)
                    normalize(it.b, it.g, sem("offset"), it.done, "x_new")
                    settle(act)
                    act.wait_ge(sem("x_new"), it.done)
                    act.dma_start(out[it.g, :, :, :], X[:, it.g, :, :]).then_inc(sem("out"), 16)
                if at(3):
                    it = at(3)
                    act.wait_ge(sem("split_rest"), it.of_layer)
                    act.copy(split[:, it.r, 1, :, :], rest[:, :, :]).then_inc(sem("split_mid"), 1)

            pipeline(act, attention_slot, 0, LAYERS)
            with act.If(not_binary(act)):
                with act.Fori(0, G) as g:
                    act.wait_ge(sem("rel_xT_ps"), g + 1)
                    act.copy(xT[:, 0, :], xT_ps[:]).then_inc(sem("rel_xT"), 1)
                    for r in range(REL):
                        act.wait_ge(sem("rel_h_ps"), g * REL + (r + 1))
                        act.copy(split[:, 0, 0, :, :], h_ps[:, :, 0:D]).then_inc(sem("rel_split_hi"), 1)
                        act.wait_ge(sem("rel_split_rest"), g * REL + (r + 2))
                        act.copy(split[:, 0, 1, :, :], rest[:, :, :]).then_inc(sem("rel_split_mid"), 1)
                    normalize(0, g, sem("rel_offset"), g + 1, "rel_x_new")
            with act.Else():
                pipeline(act, relation_slot, G * LAYERS, 1)
                act.wait_ge(sem("out"), 16 * G)

        @block.vector
        def _(dve):
            dve.memset(minus_half[:], -0.5)
            dve.memset(ones_bf[:], 1.0).then_inc(sem("ready"), 1)
            dve.memset(shift_add[:], 0.0)
            for f, value in enumerate((1 - SLOPE, -1.0, -SLOPE, -SLOPE, -1.0)):
                dve.memset(shift_k[:, f:f + 1], value)
            dve.memset(hx[:, :, :, 0:1], 1.0).then_inc(sem("ones"), 1)
            dve.wait_ge(sem("wa"), 1)
            dve.tensor_tensor(b2_ab[:, :], b2_a[:, :], ab2_sb[:, :], ALU.add).then_inc(sem("b2_ab"), 1)
            dve.wait_ge(sem("b2_ab"), 1)
            dve.wait_ge(sem("ones"), 1)
            dve.tensor_scalar(shift_add[:, 2, 0:1], b2_ab[:, 0:1], b2_ab[:, 1:2], 1 - SLOPE, ALU.add,
                              ALU.mult).then_inc(sem("shift_add"), 1)
            dve.wait_ge(sem("shift_add"), 1)

            def mask(it):
                dve.wait_ge(sem(f"adj_in{it.r}"), landed(it))
                dve.tensor_scalar(MT[:, it.g, :, :], adj_in[:, it.b, :, :], 0, None, ALU.not_equal)\
                    .then_inc(sem("mask"), 1)

            def own_max(it):
                dve.wait_ge(sem("hx"), it.done)
                if it.l == 0:
                    dve.tensor_scalar(empty_row[:, it.g, :], hx[:, it.r, :, DEG], 0.0, None, ALU.is_equal)\
                        .then_inc(sem("empty_row"), 1)
                if it.l == 1:
                    dve.tensor_scalar(col_tmp[:, it.b, R_EIGHTY, :], hx[:, it.r, :, S2], 1 - SLOPE, None,
                                      ALU.mult).then_inc(sem("r_eighty"), 1)
                s = S1 if it.l == 1 else S2
                dve.tensor_reduce(smax_own[:, it.b:it.b + 1], hx[:, it.r, :, s], AX.X, ALU.max)\
                    .then_inc(sem("smax_own"), 1)

            def node_shifts(it):
                dve.wait_ge(sem("smax_ps"), it.done)
                dve.tensor_reduce(smax[:, it.b:it.b + 1], smax_ps, AX.XY, ALU.max).then_inc(sem("smax"), 1)
                dve.wait_ge(sem("smax"), it.done)
                if it.l in (0, 2):
                    dve.scalar_tensor_tensor(out=shifts[:, it.b, :], in0=shift_k[:, 0:3],
                                             scalar=smax[:, it.b:it.b + 1], in1=shift_add[:, it.l, :],
                                             op0=ALU.mult, op1=ALU.add).then_inc(sem("shifts"), 1)
                    return
                t = col_tmp[:, it.b, :, :]
                dve.scalar_tensor_tensor(out=shifts[:, it.b, 0:2], in0=shift_k[:, 3:5],
                                         scalar=smax[:, it.b:it.b + 1], in1=shift_add[:, 1, 0:2],
                                         op0=ALU.mult, op1=ALU.add).then_inc(sem("col_shifts"), 1)
                dve.wait_ge(sem("col_shifts"), it.of_layer)
                dve.wait_ge(sem("r_eighty"), it.of_layer)
                dve.scalar_tensor_tensor(out=t[:, EXPONENT, :], in0=t[:, R_EIGHTY, :],
                                         scalar=shifts[:, it.b, 0:1],
                                         in1=shifts[:, it.b, 1:2].broadcast_to([P, C]),
                                         op0=ALU.add, op1=ALU.min).then_inc(sem("exponent"), 1)

            def node_factors(it):
                dve.wait_ge(sem("factors_raw"), halves(it))
                dve.tensor_scalar(factors[:, it.b, :, :], factors_raw[:, it.b, :, :], R_MAX, TINY, ALU.min,
                                  ALU.max).then_inc(sem("factors"), 1)
                dve.wait_ge(sem("factors"), halves(it))
                dve.tensor_scalar(neg_d[:, it.b, :], factors[:, it.b, 2, :], -1.0, None, ALU.mult)\
                    .then_inc(sem("neg_d"), 1)

            def column_terms(it):
                t = col_tmp[:, it.b, :, :]
                dve.wait_ge(sem("exponent"), it.of_layer)
                dve.tensor_tensor(t[:, BIAS, :], t[:, EXPONENT, :], col_full[:, it.g, :], ALU.mult)\
                    .then_inc(sem("col_bias"), 1)
                dve.wait_ge(sem("rows_taken"), it.of_layer)
                for c in range(C):
                    dve.scalar_tensor_tensor(out=edge[:, c, :], in0=q_rows[:, 1, :], scalar=t[:, R_EIGHTY, c:c + 1],
                                             in1=q_rows[:, 0, :], op0=ALU.subtract, op1=ALU.max)\
                        .then_inc(sem("edge_lin"), 1)

            def weights(it, cs):
                if cs[0] == 0 and (not isinstance(it.g, int) or it.l > 0 or it.g >= 2):
                    dve.wait_ge(sem("att"), it.done - 2)
                for c in cs:
                    dve.wait_ge(sem("edge"), (it.done - 1) * C + (c + 1))
                    m = MT[:, it.g, c, :]
                    if it.l == 1:
                        dve.scalar_tensor_tensor(out=PT[:, it.b, c, :], in0=m, scalar=empty_col[:, it.g, c:c + 1],
                                                 in1=edge[:, c, :], op0=ALU.max, op1=ALU.mult,
                                                 accum_out=col_tmp[:, it.b, Z, c:c + 1]).then_inc(sem("PT"), 1)
                    else:
                        extra = dict(accum_out=col_sum[:, it.b, c:c + 1]) if it.l == 0 else {}
                        dve.scalar_tensor_tensor(out=PT[:, it.b, c, :], in0=edge[:, c, :],
                                                 scalar=factors[:, it.b, 2, c:c + 1], in1=m, op0=ALU.add,
                                                 op1=ALU.mult, **extra).then_inc(sem("PT"), 1)

            def column_sums(it):
                dve.wait_ge(sem("PT"), it.done * C)
                if it.l == 0:
                    dve.tensor_scalar(empty_col[:, it.g, :], col_sum[:, it.b, :], 0.0, None, ALU.is_equal)\
                        .then_inc(sem("empty_col"), 1)
                elif it.l == 1:
                    t = col_tmp[:, it.b, :, :]
                    dve.tensor_scalar(t[:, Z, :], t[:, Z, :], TINY, None, ALU.max).then_inc(sem("z_col"), 1)
                    dve.wait_ge(sem("z_col"), it.of_layer)
                    dve.reciprocal(t[:, RZ, :], t[:, Z, :]).then_inc(sem("rz_col"), 1)

            def take_out(it):
                o = o_ps[it.b]
                dve.wait_ge(sem("att"), it.done)
                if not isinstance(it.g, int) or it.l > 0 or it.g >= 2:
                    dve.wait_ge(sem("x_new"), it.done - 2)
                if it.l in (0, 2):
                    dve.tensor_scalar(z_row[:, it.b, :], o[:, :, 0], TINY, None, ALU.max).then_inc(sem("z_row"), 1)
                    dve.wait_ge(sem("z_row"), halves(it))
                    dve.reciprocal(rz_row[:, it.b, :], z_row[:, it.b, :]).then_inc(sem("rz_row"), 1)
                    dve.wait_ge(sem("rz_row"), halves(it))
                    if it.l == 0:
                        dve.wait_ge(sem("residual"), it.done)
                    else:
                        dve.wait_ge(sem("mean_term"), it.of_layer)
                    add = residual if it.l == 0 else mean_term
                    for c in range(C):
                        last = dve.scalar_tensor_tensor(out=y[:, it.b, c, :], in0=o[:, c, 1:1 + D],
                                                        scalar=rz_row[:, it.b, c:c + 1], in1=add[:, it.b, c, :],
                                                        op0=ALU.mult, op1=ALU.add)
                    last.then_inc(sem("y_sum" if it.l == 0 else "y_lin"), 1)
                else:
                    dve.wait_ge(sem("residual"), it.done)
                    dve.tensor_tensor(y[:, it.b, :, :], o[:, :, 1:1 + D], residual[:, it.b, :, :],
                                      ALU.add).then_inc(sem("y_sum"), 1)

            def add_elu(it):
                lin = y[:, it.b, :, :]
                dve.wait_ge(sem("elu_low"), it.done - G)
                dve.scalar_tensor_tensor(out=lin, in0=lin, scalar=0.0, in1=elu_exp[:, :, :],
                                         op0=ALU.max, op1=ALU.add).then_inc(sem("y_sum"), 1)

            def moments(b, y_sem, stats_sem, done, name):
                dve.wait_ge(y_sem, done)
                for c in range(C):
                    last = dve.bn_stats(stats[:, c, :], y[:, b, c, :])
                last.then_inc(stats_sem, 1)
                settle(dve)
                dve.wait_ge(stats_sem, done)
                for c in range(C):
                    last = dve.bn_aggr(mean_var[:, b, c, :], stats[:, c, :])
                last.then_inc(sem(name + "_own"), 1)
                dve.wait_ge(sem(name + "_own"), done)
                dve.tensor_scalar(neg_mean[:, b, :], mean_var[:, b, :, 0], -1.0, None, ALU.mult)\
                    .then_inc(sem(name), 1)

            def finish(it):
                moments(it.b, sem("y_sum"), sem("stats"), it.done, "mean_var")

            def rebuild_masks():
                dve.wait_ge(sem("h_ps"), G)
                dve.wait_ge(sem("residual"), G)
                dve.sem_inc(sem("rebuild_taken"), 1)
                with dve.Fori(0, G) as g:
                    dve.wait_ge(sem("rebuild_in"), g * 32 + 32)
                    binary = square_out[:, :].rearrange("p (c i) -> p c i", c=C)
                    for side, empty in enumerate((empty_col, empty_row)):
                        if side:
                            dve.wait_ge(sem("rebuild_count"), g * 2 + 1)
                            dve.wait_ge(sem("rebuild_copied"), g + 1)
                        mark = dve.tensor_scalar(binary, adj_in[:, side, :, :], 0, None, ALU.is_gt)
                        mark.then_inc(sem("rebuild_taken" if side else "rebuild_mask"), 1)
                        if side:
                            dve.wait_ge(sem("rebuild_taken"), g + 2)
                        else:
                            dve.wait_ge(sem("rebuild_mask"), g + 1)
                            dve.tensor_copy(MT[:, g, :, :], binary).then_inc(sem("rebuild_copied"), 1)
                        dve.tensor_reduce(count[:, side, :], binary, AX.X, ALU.add).then_inc(sem("rebuild_count"), 1)
                        dve.wait_ge(sem("rebuild_count"), g * 2 + (side + 1))
                        dve.tensor_scalar(empty[:, g, :], count[:, side, :], 0.0, None, ALU.is_equal)\
                            .then_inc(sem("rebuild_done"), 1)
                dve.wait_ge(sem("rebuild_done"), 2 * G)

            def attention_slot(at, n):
                if n == G - 1:
                    with dve.If(not_binary(dve)):
                        rebuild_masks()
                    dve.wait_ge(sem("empty_col"), G)
                    dve.tensor_scalar(col_full[:, :, :], empty_col[:, :, :], -1.0, 1.0, ALU.mult, ALU.add)\
                        .then_inc(sem("col_full"), 1)
                    dve.wait_ge(sem("col_full"), 1)
                if at(2):
                    node_shifts(at(2))
                if at(1) and at(1).l == 1:
                    column_terms(at(1))
                if at(-1) and at(-1).l != 1:
                    take_out(at(-1))
                if at(-2) and at(-2).l == 2:
                    add_elu(at(-2))
                    finish(at(-2))
                if at(-1) and at(-1).l == 0:
                    finish(at(-1))
                if at(2) and at(2).l in (0, 2):
                    node_factors(at(2))
                if at(4) and at(4).l == 0:
                    mask(at(4))
                if at(1):
                    weights(at(1), (0, 1))
                if at(-1) and at(-1).l == 1:
                    finish(at(-1))
                if at(3):
                    own_max(at(3))
                if at(1):
                    weights(at(1), (2, 3))
                if at(1):
                    column_sums(at(1))
                if n == G - 3:
                    dve.wait_ge(sem("flag_sum"), G)
                    dve.tensor_reduce(flag_own[:, 0:1], flag_sum[:, :, 0], AX.X, ALU.max).then_inc(sem("flag_own"), 1)
                    dve.wait_ge(sem("flag_ps"), 1)
                    dve.tensor_reduce(flag_own[:, 1:2], xT_ps[:, 0:P], AX.X, ALU.max).then_inc(sem("flag_max"), 1)
                    dve.wait_ge(sem("flag_max"), 1)
                    dve.tensor_scalar(flag_int[:, :], flag_own[:, 1:2], 0.25 * C * N, None, ALU.is_gt)\
                        .then_inc(sem("flag"), 1)

            def relation_slot(at, n):
                if at(3):
                    it = at(3)
                    dve.wait_ge(sem("split_hi"), it.of_layer)
                    if not isinstance(it.g, int) or it.g >= 1:
                        dve.wait_ge(sem("split"), it.of_layer - 1)
                    dve.tensor_tensor(rest[:, :, :], h_ps[:, :, 0:D], split[:, it.r, 0, :, :], ALU.subtract)\
                        .then_inc(sem("split_rest"), 1)
                if at(-1):
                    take_out(at(-1))
                    finish(at(-1))
                if at(3):
                    dve.wait_ge(sem("split_mid"), it.of_layer)
                    dve.tensor_tensor(split[:, it.r, 2, :, :], rest[:, :, :], split[:, it.r, 1, :, :], ALU.subtract)\
                        .then_inc(sem("split"), 1)

            pipeline(dve, attention_slot, 0, LAYERS)
            with dve.If(not_binary(dve)):
                dve.sem_inc(sem("rel_adj_free"), 1)
                dve.sem_inc(sem("rel_x_new"), 1)
                dve.sem_inc(sem("rel_split_rest"), 1)
                with dve.Fori(0, G) as g:
                    dve.wait_ge(sem("rel_adj_in"), g * 16 + 16)
                    for r in range(REL):
                        n = g * REL + (r + 1)
                        last = dve.tensor_scalar(MT[:, g, :, :], adj_in[:, 0, :, :], r + 1, None, ALU.is_equal)
                        last.then_inc(sem("rel_mask"), 1)
                        dve.wait_ge(sem("rel_split_hi"), n)
                        dve.tensor_tensor(rest[:, :, :], h_ps[:, :, 0:D], split[:, 0, 0, :, :], ALU.subtract)\
                            .then_inc(sem("rel_split_rest"), 1)
                        dve.wait_ge(sem("rel_split_mid"), n)
                        dve.tensor_tensor(split[:, 0, 2, :, :], rest[:, :, :], split[:, 0, 1, :, :], ALU.subtract)\
                            .then_inc(sem("rel_split"), 1)
                        dve.wait_ge(sem("rel_att"), n)
                        if r == 0:
                            dve.wait_ge(sem("rel_residual"), g + 1)
                        else:
                            dve.wait_ge(sem("rel_sum"), g * (REL - 1) + r)
                        dve.tensor_tensor(y[:, 0, :, :], o_ps[0][:, :, 1:1 + D],
                                          residual[:, 0, :, :] if r == 0 else y[:, 0, :, :], ALU.add)\
                            .then_inc(sem("rel_total" if r == REL - 1 else "rel_sum"), 1)
                    dve.wait_ge(sem("rel_mask"), g * REL + REL)
                    dve.sem_inc(sem("rel_adj_free"), 1)
                    moments(0, sem("rel_total"), sem("rel_stats"), g + 1, "rel_mean_var")
            with dve.Else():
                pipeline(dve, relation_slot, G * LAYERS, 1)


def kernel(x, adj, L0_gnn_W, L0_gnn_a, L1_gnn_W, L1_gnn_a, L2_gnn_W_w, L2_gnn_W_b, L2_gnn_ai_w, L2_gnn_ai_b,
           L2_gnn_aj_w, L2_gnn_aj_b, L3_gnn_adj, L3_gnn_weight, L3_gnn_bias):
    import numpy as np
    import concourse.bacc as bacc
    from concourse.bass_utils import run_bass_kernel_spmd

    x, adj = np.asarray(x), np.asarray(adj)
    w0, w1, w2 = (np.asarray(w) for w in (L0_gnn_W, L1_gnn_W, L2_gnn_W_w))
    arrays = {
        "x": x.reshape(G, C, P, D).transpose(0, 2, 1, 3),
        "adj_by_j": adj.transpose(0, 2, 1).reshape(G, C, P, N).transpose(0, 2, 1, 3),
        "adj_by_i": adj.reshape(G, C, P, N).transpose(0, 2, 1, 3),
        "w0": w0, "w0t": w0.T, "a0": np.asarray(L0_gnn_a).reshape(2, D).T,
        "w1": w1, "w1t": w1.T, "a1": np.asarray(L1_gnn_a).reshape(2, D).T,
        "w2": w2, "w2t": w2.T,
        "a2": np.concatenate([np.asarray(L2_gnn_ai_w), np.asarray(L2_gnn_aj_w)]).T,
        "b2": np.asarray(L2_gnn_W_b),
        "ab2": np.concatenate([np.asarray(L2_gnn_ai_b), np.asarray(L2_gnn_aj_b)]),
        "w3": np.asarray(L3_gnn_weight), "b3": np.asarray(L3_gnn_bias),
    }
    arrays = {name: np.ascontiguousarray(a) for name, a in arrays.items()}
    nc = bacc.Bacc("TRN2", target_bir_lowering=False, num_devices=1)
    args = [nc.dram_tensor(name, a.shape, mybir.dt.from_np(a.dtype), kind="ExternalInput").ap()
            for name, a in arrays.items()]
    out = nc.dram_tensor("out", (G, P, C, D), F32, kind="ExternalOutput").ap()
    build(nc, *args, out)
    got = run_bass_kernel_spmd(nc, [arrays], core_ids=[0])
    return np.asarray(got.results[0]["out"]).reshape(G, P, C, D).transpose(0, 2, 1, 3).reshape(G, N, D)
```

```python
from contextlib import ExitStack

import concourse.bass as bass
from concourse import mybir

F32 = mybir.dt.float32
BF16 = mybir.dt.bfloat16
I32 = mybir.dt.int32
ALU = mybir.AluOpType
ACT = mybir.ActivationFunctionType
AX = mybir.AxisListType

P = 128
G = 16
N = 512
D = 128
C = N // P
REL = 4
EPS = 1e-5
SLOPE = 0.2
R_MAX = 5.5e34
TINY = 1e-37
LAYERS = 3
UNROLL = 4
S1, S2, DEG = 129, 130, 131
LOOP_START, LOOP_END = 4, 12
FIRST, ALL_STEPS = -4, 2 + G * (LAYERS + 1)
LAST_ATTENTION, ATTENTION_END = G * LAYERS - 4, G * LAYERS + 2
R_EIGHTY, EXPONENT, BIAS, Z, RZ = range(5)


class Item:

    def __init__(self, l, g, r):
        self.l, self.g, self.r, self.b = l, g, r % 4, r % 2
        self.done = g + (G * l + 1)
        self.of_layer = g + 1


def item(n):
    return Item(n // G, n % G, n % G) if n >= 0 else None


def build(nc, x, adj, adj_rows, w_in, w_out, a_in, b2, ab2, w3, b3, out):
    ctx = ExitStack()
    with ctx:
        def sb(name, shape, dt=F32):
            return ctx.enter_context(nc.sbuf_tensor(name, shape, dt))

        def pb(name, shape, dt=F32):
            return ctx.enter_context(nc.psum_tensor(name, shape, dt))

        sems = {}

        def sem(name):
            if name not in sems:
                sems[name] = ctx.enter_context(nc.semaphore(name))
            return sems[name]

        X = sb("X", [P, G, C, D])
        MT = sb("MT", [P, G, C, N], BF16)
        adj_in = sb("adj_in", [P, 2, C, N], I32)
        square_out = sb("square_out", [P, C * N], BF16)
        flag_sum = sb("flag_sum", [P, G, 1])
        empty_row = sb("empty_row", [P, G, C])
        empty_col = sb("empty_col", [P, G, C])
        x_cur = sb("x_cur", [P, 2, C, D])
        xT = sb("xT", [P, 2, N])
        x_sum = sb("x_sum", [P, 2])
        hx = sb("hx", [P, 4, C, 132])
        h_mean = sb("h_mean", [P, 2, D])
        h_scaled = sb("h_scaled", [P, 2, C, D])
        smax_own = sb("smax_own", [P, 2])
        smax = sb("smax", [P, 2])
        shifts = sb("shifts", [P, 2, 3])
        factors_raw = sb("factors_raw", [P, 2, 3, C])
        factors = sb("factors", [P, 2, 3, C])
        neg_d = sb("neg_d", [P, 2, C])
        q_rows = sb("q_rows", [P, 2, N])
        edge = sb("edge", [P, C, N])
        PT = sb("PT", [P, 2, C, N])
        col_tmp = sb("col_tmp", [P, 2, 5, C])
        col_full = sb("col_full", [P, G, C])
        residual = sb("residual", [P, 2, C, D])
        lin = residual
        mean_term = sb("mean_term", [P, 2, C, D])
        z_row = sb("z_row", [P, 2, C])
        rz_row = sb("rz_row", [P, 2, C])
        y = sb("y", [P, 2, C, D])
        elu_exp = sb("elu_exp", [P, C, D])
        stats = sb("stats", [P, C, 6])
        mean_var = sb("mean_var", [P, 2, C, 2])
        var_eps = sb("var_eps", [P, 2, C])
        rstd = sb("rstd", [P, 2, C])
        neg_mean = sb("neg_mean", [P, 2, C])
        offset = sb("offset", [P, 2, C])
        elu_low_arg = sb("elu_low_arg", [P, C, D])
        centered = sb("centered", [P, C, D])
        split = sb("split", [P, 4, 3, C, D], BF16)
        rest = sb("rest", [P, C, D])
        elu_high = rest
        ident = sb("ident", [P, P])
        ones_bf = sb("ones_bf", [P, 1], BF16)
        col_sum = sb("col_sum", [P, 2, C])
        count = sb("count", [P, 2, C])
        flag_own = sb("flag_own", [P, 2])
        neg_half = sb("neg_half", [P, C])
        eps_tile = sb("eps_tile", [P, C])
        minus_one = sb("minus_one", [P, C])
        minus_half = sb("minus_half", [P, 1])
        wx = sb("wx", [P, 3, 130])
        w_back = sb("w_back", [P, 3, D])
        a_cols = sb("a_cols", [P, 3, 2])
        w_rel = sb("w_rel", [P, REL, D])
        bias2 = sb("bias2", [P, D])
        bias2_less_one = sb("bias2_less_one", [P, D])
        bias2_col = sb("bias2_col", [P, 1])
        bias3 = sb("bias3", [P, D])
        ab2_sb = sb("ab2_sb", [P, 2])
        shift_k = sb("shift_k", [P, 5])
        b2_a = sb("b2_a", [P, 2])
        b2_ab = sb("b2_ab", [P, 2])
        shift_add = sb("shift_add", [P, LAYERS, 3])
        flag_int = sb("flag_int", [P, 1], I32)

        xT_ps = pb("xT_ps", [P, N])
        h_ps = pb("h_ps", [P, C, 256])
        rows_ps = pb("rows_ps", [P, N])
        o_ps = [pb(f"o_ps{b}", [P, C, 256]) for b in range(2)]
        h_mean_ps = h_ps[:, 2:4, 132:196]
        smax_ps = h_ps[:, 0:2, 132:196]

        block = ctx.enter_context(nc.Block())

        def pipeline(eng, slot, begin, end, items):
            n = begin
            while n < end:
                if n >= 0 and n % G == LOOP_START:
                    l = n // G
                    with eng.Fori(LOOP_START, LOOP_END - UNROLL + 1, UNROLL) as i:
                        for u in range(UNROLL):
                            slot(lambda k, u=u: Item(l, i + (u + k), u + k + 4), None)
                    n += LOOP_END - LOOP_START
                else:
                    slot(lambda k, n=n: item(n + k) if n + k < items else None, n)
                    n += 1

        def last_layers(attention_slot, relation_slot):
            def slot(at, n):
                if n is not None and n < ATTENTION_END:
                    attention_slot(lambda k: at(k) if at(k) and at(k).l < LAYERS else None, n)
                relation_slot(lambda k: at(k) if at(k) and at(k).l == LAYERS else None, n)
            return slot

        def halves(it):
            return it.of_layer + (G if it.l == 2 else 0)

        def landed(it):
            return 16 * (it.g // 4 + 1) if isinstance(it.g, int) else it.g * 4 + (16 - 4 * it.r)

        def settle(eng):
            eng.wait_ge(sem("ready"), 1)

        def not_binary(eng):
            eng.wait_ge(sem("flag"), 1)
            return eng.value_load(flag_int[0:1, 0:1], min_val=0, max_val=1) > 0

        @block.sync
        def _(sp):

            def load(it):
                settle(sp)
                if not isinstance(it.g, int) or it.g >= 2:
                    sp.wait_ge(sem("mask"), it.of_layer - 2)
                    sp.wait_ge(sem("flag_sum"), it.of_layer - 2)
                sp.dma_start(adj_in[:, it.b, :, :], adj[it.g, :, :, :]).then_inc(sem(f"adj_in{it.r}"), 16)

            def load_x(it):
                sp.dma_start(X[:, it.g, :, :], x[it.g, :, :, :]).then_inc(sem(f"x_in{it.r}"), 16)

            def copy_x(it):
                settle(sp)
                if not isinstance(it.g, int) or it.l > 0 or it.g >= 2:
                    sp.wait_ge(sem("xT_ps"), it.done - 2)
                sp.dma_start(x_cur[:, it.b, :, :], x[it.g, :, :, :] if it.l == 0 else X[:, it.g, :, :])\
                    .then_inc(sem(f"x_cur{it.r}"), 16)

            def copy_layer(l):
                with sp.Fori(0, G - UNROLL + 1, UNROLL) as i:
                    for u in range(UNROLL):
                        copy_x(Item(l, i + u, u))

            copy_x(item(0))
            load(item(0))
            copy_x(item(1))
            load(item(1))
            load_x(item(0))
            load_x(item(1))
            for n in (2, 3):
                copy_x(item(n))
                load(item(n))
                load_x(item(n))
            sp.dma_start(w_rel[:, :, :], w3.rearrange("r d o -> d r o")).then_inc(sem("w_late"), 16)
            sp.dma_start(bias3[:, :], b3.partition_broadcast(P)).then_inc(sem("w_late"), 16)
            with sp.Fori(4, G - UNROLL + 1, UNROLL) as i:
                for u in range(UNROLL):
                    copy_x(Item(0, i + u, u))
                    load(Item(0, i + u, u))
                    load_x(Item(0, i + u, u))
            for n in range(G, G + 3):
                copy_x(item(n))
            with sp.If(not_binary(sp)):
                with sp.Fori(0, G) as g:
                    settle(sp)
                    sp.wait_ge(sem("rebuild_taken"), g + 1)
                    sp.dma_start(adj_in[:, 0, :, :], adj[g, :, :, :]).then_inc(sem("rebuild_in"), 16)
                    sp.dma_start(adj_in[:, 1, :, :], adj_rows[g, :, :, :]).then_inc(sem("rebuild_in"), 16)
            copy_x(item(G + 3))
            with sp.Fori(4, G - UNROLL + 1, UNROLL) as i:
                for u in range(UNROLL):
                    copy_x(Item(1, i + u, u))
            copy_layer(2)

            with sp.If(not_binary(sp)):
                with sp.Fori(0, G) as g:
                    settle(sp)
                    sp.wait_ge(sem("rel_adj_free"), g + 1)
                    sp.dma_start(adj_in[:, 0, :, :], adj[g, :, :, :]).then_inc(sem("rel_adj_in"), 16)
                with sp.Fori(0, G) as g:
                    settle(sp)
                    sp.wait_ge(sem("rel_x_new"), g + 2)
                    sp.dma_start(out[g, :, :, :], X[:, g, :, :]).then_inc(sem("rel_out"), 16)
                sp.wait_ge(sem("rel_out"), 16 * G)
            with sp.Else():
                copy_layer(LAYERS)

        W_IN = 16 * 6

        @block.gpsimd
        def _(pool):
            pool.memset(ident[:], 0.0).then_inc(sem("ident_zero"), 1)
            pool.wait_ge(sem("ident_zero"), 1)
            pool.affine_select(out=ident[:], in_=ident[:], compare_op=ALU.not_equal, fill=1.0, base=0,
                               pattern=[[-1, P]], channel_multiplier=1).then_inc(sem("ident"), 1)
            pool.memset(neg_half[:], -0.5)
            pool.memset(eps_tile[:], EPS)
            pool.memset(minus_one[:], -1.0).then_inc(sem("pool_const"), 1)
            pool.wait_ge(sem("pool_const"), 1)

            def mean(it):
                settle(pool)
                if it.l == 2:
                    if not isinstance(it.g, int) or it.g >= 2:
                        pool.wait_ge(sem("y_lin"), it.of_layer - 2)
                elif not isinstance(it.g, int) or it.g >= 2:
                    pool.wait_ge(sem("residual"), it.done - 2)
                pool.wait_ge(sem("h_mean"), halves(it))
                if it.l == 0:
                    pool.wait_ge(sem("empty_row"), it.of_layer)
                pool.tensor_tensor(mean_term[:, it.b, :, :],
                                   h_mean[:, it.b, :].unsqueeze(1).broadcast_to([P, C, D]),
                                   empty_row[:, it.g, :].unsqueeze(2).broadcast_to([P, C, D]),
                                   ALU.mult).then_inc(sem("mean_raw"), 1)
                if it.l == 2:
                    settle(pool)
                    pool.wait_ge(sem("mean_raw"), halves(it))
                    pool.tensor_tensor(mean_term[:, it.b, :, :], mean_term[:, it.b, :, :],
                                       bias2_less_one[:, :].unsqueeze(1).broadcast_to([P, C, D]),
                                       ALU.add).then_inc(sem("mean_term"), 1)

            def add_residual(it):
                settle(pool)
                if not isinstance(it.g, int) or it.g >= 2:
                    pool.wait_ge(sem("y_sum"), it.done - 2)
                pool.wait_ge(sem(f"x_in{it.r}"), landed(it))
                settle(pool)
                pool.wait_ge(sem("mean_raw"), it.done)
                pool.tensor_tensor(residual[:, it.b, :, :], X[:, it.g, :, :], mean_term[:, it.b, :, :],
                                   ALU.add).then_inc(sem("residual"), 1)

            def scale_h(it):
                pool.wait_ge(sem("rz_col"), it.of_layer)
                pool.wait_ge(sem("att"), it.done - 2)
                pool.tensor_tensor(h_scaled[:, it.b, :, :], hx[:, it.r, :, 1:1 + D],
                                   col_tmp[:, it.b, RZ, :].unsqueeze(2).broadcast_to([P, C, D]),
                                   ALU.mult).then_inc(sem("h_scaled"), 1)

            def find_rstd(it):
                pool.wait_ge(sem("mean_var"), it.done)
                pool.tensor_tensor(var_eps[:, it.b, :], mean_var[:, it.b, :, 1], eps_tile[:], ALU.add)\
                    .then_inc(sem("var_eps"), 1)
                pool.wait_ge(sem("var_eps"), it.done)
                pool.tensor_tensor(rstd[:, it.b, :], var_eps[:, it.b, :], neg_half[:], ALU.pow)\
                    .then_inc(sem("rstd"), 1)

            def find_offset(it):
                pool.tensor_tensor(neg_mean[:, it.b, :], mean_var[:, it.b, :, 0], minus_one[:], ALU.mult)\
                    .then_inc(sem("neg_mean"), 1)
                pool.wait_ge(sem("rstd"), it.done)
                pool.wait_ge(sem("neg_mean"), it.of_layer)
                pool.tensor_tensor(offset[:, it.b, :], neg_mean[:, it.b, :], rstd[:, it.b, :], ALU.mult)\
                    .then_inc(sem("offset"), 1)

            def normalize(it):
                if not isinstance(it.g, int) or it.l > 0 or it.g >= 1:
                    pool.wait_ge(sem("x_new"), it.done - 1)
                pool.tensor_tensor(centered[:, :, :], y[:, it.b, :, :],
                                   mean_var[:, it.b, :, 0].unsqueeze(2).broadcast_to([P, C, D]),
                                   ALU.subtract).then_inc(sem("centered"), 1)
                settle(pool)
                pool.wait_ge(sem("centered"), it.done)
                pool.wait_ge(sem("rstd"), it.done)
                pool.tensor_tensor(X[:, it.g, :, :], centered[:, :, :],
                                   rstd[:, it.b, :].unsqueeze(2).broadcast_to([P, C, D]),
                                   ALU.mult).then_inc(sem("x_new"), 1)

            def elu_low(it):
                settle(pool)
                pool.wait_ge(sem("elu_exp"), it.done - G)
                pool.tensor_tensor(elu_exp[:, :, :], elu_exp[:, :, :], X[:, it.g, :, :], ALU.add)\
                    .then_inc(sem("elu_low"), 1)
                if it.l == 1:
                    pool.wait_ge(sem("elu_high"), it.of_layer)
                    pool.wait_ge(sem("elu_low"), it.of_layer)
                    pool.tensor_tensor(y[:, it.b, :, :], elu_high[:, :, :], elu_exp[:, :, :], ALU.add)\
                        .then_inc(sem("y_sum"), 1)

            def attention_slot(at, n):
                if at(-1) and at(-1).l == 1:
                    elu_low(at(-1))
                if at(1) and at(1).l != 1:
                    mean(at(1))
                if at(-1) and at(-1).l == 2:
                    elu_low(at(-1))
                if at(-2) and at(-2).l == 2:
                    find_rstd(at(-2))
                if at(-2):
                    normalize(at(-2))
                if at(-1) and at(-1).l != 2:
                    find_rstd(at(-1))
                if at(1) and at(1).l == 0:
                    add_residual(at(1))
                if at(1) and at(1).l == 1:
                    scale_h(at(1))

            def relation_slot(at, n):
                if at(1):
                    it = at(1)
                    settle(pool)
                    pool.wait_ge(sem("y_sum"), it.done - 2)
                    pool.tensor_tensor(residual[:, it.b, :, :], X[:, it.g, :, :],
                                       bias3[:, :].unsqueeze(1).broadcast_to([P, C, D]),
                                       ALU.add).then_inc(sem("residual"), 1)
                if at(-1):
                    find_rstd(at(-1))
                    find_offset(at(-1))

            pipeline(pool, attention_slot, FIRST, LAST_ATTENTION, G * LAYERS)
            pool.wait_ge(sem("w_late"), 32)
            with pool.If(not_binary(pool)):
                pipeline(pool, attention_slot, LAST_ATTENTION, ATTENTION_END, G * LAYERS)
                with pool.Fori(0, G) as g:
                    pool.wait_ge(sem("x_new"), g + (G * 2 + 1))
                    pool.wait_ge(sem("rel_x_new"), g + 1)
                    pool.tensor_copy(x_cur[:, 0, :, :], X[:, g, :, :]).then_inc(sem("rel_x_cur"), 1)
                    pool.tensor_tensor(residual[:, 0, :, :], X[:, g, :, :],
                                       bias3[:, :].unsqueeze(1).broadcast_to([P, C, D]),
                                       ALU.add).then_inc(sem("rel_residual"), 1)
                    pool.wait_ge(sem("rel_mean_var"), g + 1)
                    pool.tensor_tensor(neg_mean[:, 0, :], mean_var[:, 0, :, 0], minus_one[:], ALU.mult)\
                        .then_inc(sem("rel_neg_mean"), 1)
                    pool.tensor_tensor(var_eps[:, 0, :], mean_var[:, 0, :, 1], eps_tile[:], ALU.add)\
                        .then_inc(sem("rel_var_eps"), 1)
                    pool.wait_ge(sem("rel_var_eps"), g + 1)
                    pool.tensor_tensor(rstd[:, 0, :], var_eps[:, 0, :], neg_half[:], ALU.pow)\
                        .then_inc(sem("rel_rstd"), 1)
                    pool.wait_ge(sem("rel_neg_mean"), g + 1)
                    pool.wait_ge(sem("rel_rstd"), g + 1)
                    pool.tensor_tensor(offset[:, 0, :], neg_mean[:, 0, :], rstd[:, 0, :], ALU.mult)\
                        .then_inc(sem("rel_offset"), 1)
            with pool.Else():
                pipeline(pool, last_layers(attention_slot, relation_slot), LAST_ATTENTION, ALL_STEPS, G * (LAYERS + 1))

        @block.tensor
        def _(pe):
            pe.wait_ge(sem("w_in"), W_IN)
            for l in range(LAYERS):
                pe.matmul(xT_ps[:, 2 * l:2 * l + 2], w_back[:, l, :], a_cols[:, l, :], start=True, stop=True)
            pe.matmul(xT_ps[:, 6:8], bias2_col[:, 0:1].broadcast_to([P, P]), a_cols[:, 2, :],
                      start=True, stop=True).then_inc(sem("wa_ps"), 1)
            pe.wait_ge(sem("ident"), 1)
            pe.wait_ge(sem("wa"), 1)
            pe.wait_ge(sem("ones"), 1)

            def transpose_x(x_sem, done, b):
                pe.wait_ge(x_sem, done)
                for c in range(C):
                    last = pe.transpose(xT_ps[:, c * P:(c + 1) * P], x_cur[:, b, c, :], ident[:])
                return last

            def next_transpose(it):
                if not isinstance(it.g, int) or it.l > 0 or it.g >= 1:
                    pe.wait_ge(sem("xT"), it.done - 1)
                transpose_x(sem(f"x_cur{it.r}"), landed(it) + 4 * G * it.l, it.b).then_inc(sem("xT_ps"), 1)

            def project(it):
                pe.wait_ge(sem("xT"), it.done)
                if it.l < LAYERS:
                    if not isinstance(it.g, int) or it.l > 0 or it.g >= 1:
                        pe.wait_ge(sem("hx"), it.done - 1)
                        pe.wait_ge(sem("smax"), it.done - 1)
                elif not isinstance(it.g, int) or it.g >= 1:
                    pe.wait_ge(sem("split_rest"), it.of_layer - 1)
                else:
                    pe.wait_ge(sem("hx"), it.done - 1)
                    pe.wait_ge(sem("smax"), it.done - 1)
                if it.l == 0:
                    pe.wait_ge(sem("mask"), it.of_layer)
                for c in range(C):
                    lhsT = xT[:, it.b, c * P:(c + 1) * P]
                    if it.l < LAYERS:
                        last = pe.matmul(h_ps[:, c, 0:130], lhsT, wx[:, it.l, :], start=True, stop=True)
                    else:
                        last = pe.matmul(h_ps[:, c, 0:D], lhsT, w_rel[:, 0, :], start=True, stop=True)
                if it.l in (0, 2):
                    for e in range(2):
                        last = pe.matmul(h_mean_ps[:, e, :], x_sum[:, it.b:it.b + 1].broadcast_to([P, P]),
                                         wx[:, it.l, e * 64:(e + 1) * 64], start=True, stop=True)
                if it.l == 0:
                    for ic in range(C):
                        for jc in range(C):
                            last = pe.matmul(h_ps[:, ic, 130:131], MT[:, it.g, jc, ic * P:(ic + 1) * P],
                                             ones_bf[:, 0:1], start=(jc == 0), stop=(jc == C - 1))
                last.then_inc(sem("h_ps"), 1)

            def spread_max(it):
                pe.wait_ge(sem("smax_own"), it.done)
                pe.transpose(smax_ps, smax_own[:, it.b:it.b + 1].broadcast_to([P, P]), ident[:])\
                    .then_inc(sem("smax_ps"), 1)

            def spread_rows(it):
                if it.l == 1:
                    pe.wait_ge(sem("hx"), it.done)
                else:
                    pe.wait_ge(sem("factors"), halves(it))
                if not isinstance(it.g, int) or it.l > 0 or it.g >= 1:
                    pe.wait_ge(sem("edge"), (it.done - 1) * C)
                for c in range(C):
                    col = hx[:, it.r, c, S1:S1 + 1] if it.l == 1 else factors[:, it.b, 0, c:c + 1]
                    last = pe.transpose(rows_ps[:, c * P:(c + 1) * P], col.broadcast_to([P, P]), ident[:])
                last.then_inc(sem("rows_ps"), 1)

            def attend(it):
                pe.wait_ge(sem("PT"), it.done * C)
                if it.l == 1:
                    pe.wait_ge(sem("h_scaled"), it.of_layer)
                for ic in range(C):
                    for jc in range(C):
                        lhsT = PT[:, it.b, jc, ic * P:(ic + 1) * P]
                        if it.l == 1:
                            last = pe.matmul(o_ps[it.b][:, ic, 1:1 + D], lhsT, h_scaled[:, it.b, jc, :],
                                             start=(jc == 0), stop=(jc == C - 1))
                        else:
                            last = pe.matmul(o_ps[it.b][:, ic, 0:1 + D], lhsT, hx[:, it.r, jc, 0:1 + D],
                                             start=(jc == 0), stop=(jc == C - 1))
                last.then_inc(sem("att"), 1)

            def attention_slot(at, n):
                if at(1):
                    spread_rows(at(1))
                if at(2):
                    spread_max(at(2))
                if n == G - 2:
                    pe.wait_ge(sem("flag_own"), 1)
                    pe.wait_ge(sem("xT"), at(3).done)
                    pe.transpose(xT_ps[:, 0:P], flag_own[:, 0:1].broadcast_to([P, P]), ident[:])\
                        .then_inc(sem("flag_ps"), 1)
                    pe.wait_ge(sem("flag_max"), 1)
                if at(4):
                    next_transpose(at(4))
                if at(3):
                    project(at(3))
                if at(0):
                    attend(at(0))

            def relate(o, g, r, first, final):
                for ic in range(C):
                    for jc in range(C):
                        for part in range(3):
                            last = pe.matmul(o[:, ic, 1:1 + D], MT[:, g, jc, ic * P:(ic + 1) * P],
                                             split[:, r, part, jc, :], start=(first and jc == 0 and part == 0),
                                             stop=(final and jc == C - 1 and part == 2),
                                             skip_group_check=not (first and final))
                return last

            def relation_slot(at, n):
                if at(4):
                    next_transpose(at(4))
                if at(3):
                    project(at(3))
                if at(0):
                    it = at(0)
                    pe.wait_ge(sem("split"), it.of_layer)
                    if isinstance(it.g, int) and it.g < 2:
                        pe.wait_ge(sem("y_lin"), G - 1 + it.g)
                    else:
                        pe.wait_ge(sem("y_sum"), it.done - 2)
                    relate(o_ps[it.b], it.g, it.r, True, True).then_inc(sem("att"), 1)

            pipeline(pe, attention_slot, FIRST, LAST_ATTENTION, G * LAYERS)
            pe.wait_ge(sem("w_late"), 32)
            with pe.If(not_binary(pe)):
                pipeline(pe, attention_slot, LAST_ATTENTION, ATTENTION_END, G * LAYERS)
                pe.wait_ge(sem("y_sum"), G * LAYERS)
                with pe.Fori(0, G) as g:
                    transpose_x(sem("rel_x_cur"), g + 1, 0).then_inc(sem("rel_xT_ps"), 1)
                    pe.wait_ge(sem("rel_xT"), g + 1)
                    for r in range(REL):
                        pe.wait_ge(sem("rel_split_rest"), g * REL + (r + 1))
                        for c in range(C):
                            last = pe.matmul(h_ps[:, c, 0:D], xT[:, 0, c * P:(c + 1) * P], w_rel[:, r, :],
                                             start=True, stop=True)
                        last.then_inc(sem("rel_h_ps"), 1)
                        pe.wait_ge(sem("rel_split"), g * REL + (r + 1))
                        pe.wait_ge(sem("rel_mask"), g * REL + (r + 1))
                        relate(o_ps[0], g, 0, True, True).then_inc(sem("rel_att"), 1)
            with pe.Else():
                pipeline(pe, last_layers(attention_slot, relation_slot), LAST_ATTENTION, ALL_STEPS, G * (LAYERS + 1))

        @block.scalar
        def _(act):
            act.dma_start(wx[:, :, 0:D], w_in).then_inc(sem("w_in"), 16)
            act.dma_start(w_back[:, :, :], w_out).then_inc(sem("w_in"), 16)
            act.dma_start(a_cols[:, :, :], a_in).then_inc(sem("w_in"), 16)
            act.dma_start(bias2_col[:, :], b2.rearrange("(p o) -> p o", o=1)).then_inc(sem("w_in"), 16)
            act.dma_start(bias2[:, :], b2.partition_broadcast(P)).then_inc(sem("w_in"), 16)
            act.dma_start(ab2_sb[:, :], ab2.partition_broadcast(P)).then_inc(sem("w_in"), 16)
            act.wait_ge(sem("wa_ps"), 1)
            for l in range(LAYERS):
                act.copy(wx[:, l, D:D + 2], xT_ps[:, 2 * l:2 * l + 2])
            act.copy(b2_a[:, :], xT_ps[:, 6:8]).then_inc(sem("wa"), 1)
            act.wait_ge(sem("ones"), 1)

            def take_xT(it):
                act.wait_ge(sem("xT_ps"), it.done)
                if not isinstance(it.g, int) or it.l > 0 or it.g >= 2:
                    act.wait_ge(sem("h_ps"), it.done - 2)
                extra = dict(accum_out=x_sum[:, it.b:it.b + 1]) if it.l in (0, 2) else {}
                act.activation(xT[:, it.b, :], xT_ps[:], ACT.Copy, **extra).then_inc(sem("xT"), 1)

            def take_h(it):
                act.wait_ge(sem("h_ps"), it.done)
                if it.l == LAYERS:
                    act.copy(split[:, it.r, 0, :, :], h_ps[:, :, 0:D]).then_inc(sem("split_hi"), 1)
                    return
                if it.l in (0, 2):
                    if not isinstance(it.g, int) or it.l > 0 or it.g >= 2:
                        act.wait_ge(sem("mean_raw"), halves(it) - 2)
                    act.activation(h_mean[:, it.b, :].rearrange("p (e d) -> p e d", e=2), h_mean_ps, ACT.Copy,
                                   scale=1.0 / N).then_inc(sem("h_mean"), 1)
                width = 131 if it.l == 0 else 130
                act.copy(hx[:, it.r, :, 1:1 + width], h_ps[:, :, 0:width]).then_inc(sem("hx"), 1)

            def node_factors(it):
                act.wait_ge(sem("shifts"), halves(it))
                for f, (s, scale) in enumerate(((S1, 1 - SLOPE), (S2, 1.0), (S2, SLOPE))):
                    last = act.activation(factors_raw[:, it.b, f, :], hx[:, it.r, :, s], ACT.Exp,
                                          scale=scale, bias=shifts[:, it.b, f:f + 1])
                last.then_inc(sem("factors_raw"), 1)

            def take_rows(it):
                act.wait_ge(sem("rows_ps"), it.done)
                if not isinstance(it.g, int) or it.g >= 1:
                    act.wait_ge(sem("edge_lin"), (it.of_layer - 1) * C)
                act.copy(q_rows[:, 0, :], rows_ps[:])
                act.activation(q_rows[:, 1, :], rows_ps[:], ACT.Copy, scale=SLOPE).then_inc(sem("rows_taken"), 1)

            def edges(it, cs):
                if cs[0] == 0:
                    if it.l == 1:
                        act.wait_ge(sem("col_bias"), it.of_layer)
                    else:
                        act.wait_ge(sem("rows_ps"), it.done)
                        act.wait_ge(sem("neg_d"), halves(it))
                for c in cs:
                    if it.l == 1:
                        act.wait_ge(sem("edge_lin"), (it.of_layer - 1) * C + (c + 1))
                        act.activation(edge[:, c, :], edge[:, c, :], ACT.Exp, bias=col_tmp[:, it.b, BIAS, c:c + 1],
                                       scale=col_full[:, it.g, c:c + 1]).then_inc(sem("edge"), 1)
                    else:
                        if not isinstance(it.g, int) or it.l > 0 or it.g >= 1:
                            act.wait_ge(sem("PT"), (it.done - 2) * C + (c + 1))
                        act.activation(edge[:, c, :], rows_ps[:], ACT.Relu, bias=neg_d[:, it.b, c:c + 1],
                                       scale=factors[:, it.b, 1, c:c + 1]).then_inc(sem("edge"), 1)

            def elu(it):
                if not isinstance(it.g, int) or it.l > 1 or it.g >= 1:
                    act.wait_ge(sem("elu_exp"), it.done - (G + 1))
                if it.l == 1:
                    act.wait_ge(sem("att"), it.done)
                    lin_ps = o_ps[it.b][:, :, 1:1 + D]
                    act.activation(elu_low_arg[:, :, :], lin_ps, ACT.Relu, scale=-1.0)\
                        .then_inc(sem("elu_low_arg"), 1)
                    act.wait_ge(sem("y_sum"), it.done - 1)
                    act.activation(elu_high[:, :, :], lin_ps, ACT.Relu).then_inc(sem("elu_high_raw"), 1)
                else:
                    act.wait_ge(sem("y_lin"), it.of_layer)
                    act.activation(elu_low_arg[:, :, :], lin[:, it.b, :, :], ACT.Relu, scale=-1.0,
                                   bias=minus_one[:, 0:1]).then_inc(sem("elu_low_arg"), 1)
                    act.wait_ge(sem("y_sum"), it.done - 1)
                act.wait_ge(sem("elu_low_arg"), it.done - G)
                act.activation(elu_exp[:, :, :], elu_low_arg[:, :, :], ACT.Exp, scale=-1.0)\
                    .then_inc(sem("elu_exp"), 1)
                if it.l == 1:
                    act.wait_ge(sem("elu_high_raw"), it.of_layer)
                    act.activation(elu_high[:, :, :], elu_high[:, :, :], ACT.Identity, bias=minus_one[:, 0:1])\
                        .then_inc(sem("elu_high"), 1)

            def normalize(b, g, offset_sem, done, name):
                act.wait_ge(offset_sem, done)
                for c in range(C):
                    last = act.activation(X[:, g, c, :], y[:, b, c, :], ACT.Identity, bias=offset[:, b, c:c + 1],
                                          scale=rstd[:, b, c:c + 1])
                last.then_inc(sem(name), 1)

            def flag(it):
                act.wait_ge(sem(f"adj_in{it.r}"), landed(it))
                if not isinstance(it.g, int) or it.g >= 1:
                    act.wait_ge(sem("flag_sum"), it.of_layer - 1)
                act.activation(square_out[:, :], adj_in[:, it.b, :, :].rearrange("p c i -> p (c i)"), ACT.Square,
                               bias=minus_half[:, 0:1], accum_out=flag_sum[:, it.g, :])\
                    .then_inc(sem("flag_sum"), 1)

            def attention_slot(at, n):
                if at(1) and at(1).l == 1:
                    take_rows(at(1))
                if at(-1) and at(-1).l == 1:
                    elu(at(-1))
                if at(1):
                    edges(at(1), (0, 1))
                if at(2) and at(2).l in (0, 2):
                    node_factors(at(2))
                if at(-1) and at(-1).l == 2:
                    elu(at(-1))
                if at(1):
                    edges(at(1), (2, 3))
                if at(3):
                    take_h(at(3))
                if at(4):
                    take_xT(at(4))
                if at(4) and at(4).l == 0:
                    flag(at(4))

            def relation_slot(at, n):
                if at(4):
                    take_xT(at(4))
                if at(3):
                    take_h(at(3))
                if at(-2):
                    it = at(-2)
                    if n == G * LAYERS + 2:
                        act.wait_ge(sem("x_new"), G * LAYERS)
                    normalize(it.b, it.g, sem("offset"), it.of_layer, "x_new")
                    settle(act)
                    act.wait_ge(sem("x_new"), it.done)
                    act.dma_start(out[it.g, :, :, :], X[:, it.g, :, :]).then_inc(sem("out"), 16)
                if at(3):
                    it = at(3)
                    act.wait_ge(sem("split_rest"), it.of_layer)
                    act.copy(split[:, it.r, 1, :, :], rest[:, :, :]).then_inc(sem("split_mid"), 1)

            pipeline(act, attention_slot, FIRST, LAST_ATTENTION, G * LAYERS)
            with act.If(not_binary(act)):
                pipeline(act, attention_slot, LAST_ATTENTION, ATTENTION_END, G * LAYERS)
                with act.Fori(0, G) as g:
                    act.wait_ge(sem("rel_xT_ps"), g + 1)
                    act.copy(xT[:, 0, :], xT_ps[:]).then_inc(sem("rel_xT"), 1)
                    for r in range(REL):
                        act.wait_ge(sem("rel_h_ps"), g * REL + (r + 1))
                        act.copy(split[:, 0, 0, :, :], h_ps[:, :, 0:D]).then_inc(sem("rel_split_hi"), 1)
                        act.wait_ge(sem("rel_split_rest"), g * REL + (r + 2))
                        act.copy(split[:, 0, 1, :, :], rest[:, :, :]).then_inc(sem("rel_split_mid"), 1)
                    normalize(0, g, sem("rel_offset"), g + 1, "rel_x_new")
            with act.Else():
                pipeline(act, last_layers(attention_slot, relation_slot), LAST_ATTENTION, ALL_STEPS, G * (LAYERS + 1))
                act.wait_ge(sem("out"), 16 * G)

        @block.vector
        def _(dve):
            dve.memset(minus_half[:], -0.5)
            dve.memset(ones_bf[:], 1.0).then_inc(sem("ready"), 1)
            dve.memset(shift_add[:], 0.0)
            for f, value in enumerate((1 - SLOPE, -1.0, -SLOPE, -SLOPE, -1.0)):
                dve.memset(shift_k[:, f:f + 1], value)
            dve.memset(hx[:, :, :, 0:1], 1.0).then_inc(sem("ones"), 1)
            dve.wait_ge(sem("wa"), 1)
            dve.tensor_scalar(bias2_less_one[:, :], bias2[:, :], -1.0, None, ALU.add)
            dve.tensor_tensor(b2_ab[:, :], b2_a[:, :], ab2_sb[:, :], ALU.add).then_inc(sem("b2_ab"), 1)
            dve.wait_ge(sem("b2_ab"), 1)
            dve.wait_ge(sem("ones"), 1)
            dve.tensor_scalar(shift_add[:, 2, 0:1], b2_ab[:, 0:1], b2_ab[:, 1:2], 1 - SLOPE, ALU.add,
                              ALU.mult).then_inc(sem("shift_add"), 1)
            dve.wait_ge(sem("shift_add"), 1)

            def mask(it):
                dve.wait_ge(sem(f"adj_in{it.r}"), landed(it))
                dve.tensor_scalar(MT[:, it.g, :, :], adj_in[:, it.b, :, :], 0, None, ALU.not_equal)\
                    .then_inc(sem("mask"), 1)

            def own_max(it):
                dve.wait_ge(sem("hx"), it.done)
                if it.l == 0:
                    dve.tensor_scalar(empty_row[:, it.g, :], hx[:, it.r, :, DEG], 0.0, None, ALU.is_equal)\
                        .then_inc(sem("empty_row"), 1)
                if it.l == 1:
                    dve.tensor_scalar(col_tmp[:, it.b, R_EIGHTY, :], hx[:, it.r, :, S2], 1 - SLOPE, None,
                                      ALU.mult).then_inc(sem("r_eighty"), 1)
                s = S1 if it.l == 1 else S2
                dve.tensor_reduce(smax_own[:, it.b:it.b + 1], hx[:, it.r, :, s], AX.X, ALU.max)\
                    .then_inc(sem("smax_own"), 1)

            def take_max(it):
                dve.wait_ge(sem("smax_ps"), it.done)
                dve.tensor_reduce(smax[:, it.b:it.b + 1], smax_ps, AX.XY, ALU.max).then_inc(sem("smax"), 1)

            def node_shifts(it):
                dve.wait_ge(sem("smax"), it.done)
                if it.l in (0, 2):
                    dve.scalar_tensor_tensor(out=shifts[:, it.b, :], in0=shift_k[:, 0:3],
                                             scalar=smax[:, it.b:it.b + 1], in1=shift_add[:, it.l, :],
                                             op0=ALU.mult, op1=ALU.add).then_inc(sem("shifts"), 1)
                else:
                    dve.scalar_tensor_tensor(out=shifts[:, it.b, 0:2], in0=shift_k[:, 3:5],
                                             scalar=smax[:, it.b:it.b + 1], in1=shift_add[:, 1, 0:2],
                                             op0=ALU.mult, op1=ALU.add).then_inc(sem("col_shifts"), 1)

            def exponents(it):
                t = col_tmp[:, it.b, :, :]
                dve.wait_ge(sem("col_shifts"), it.of_layer)
                dve.wait_ge(sem("r_eighty"), it.of_layer)
                dve.scalar_tensor_tensor(out=t[:, EXPONENT, :], in0=t[:, R_EIGHTY, :],
                                         scalar=shifts[:, it.b, 0:1],
                                         in1=shifts[:, it.b, 1:2].broadcast_to([P, C]),
                                         op0=ALU.add, op1=ALU.min).then_inc(sem("exponent"), 1)

            def node_factors(it):
                dve.wait_ge(sem("factors_raw"), halves(it))
                dve.tensor_scalar(factors[:, it.b, :, :], factors_raw[:, it.b, :, :], R_MAX, TINY, ALU.min,
                                  ALU.max).then_inc(sem("factors"), 1)
                dve.tensor_scalar(neg_d[:, it.b, :], factors_raw[:, it.b, 2, :], -1.0, -TINY, ALU.mult, ALU.min)\
                    .then_inc(sem("neg_d"), 1)

            def column_terms(it):
                t = col_tmp[:, it.b, :, :]
                dve.wait_ge(sem("exponent"), it.of_layer)
                dve.tensor_tensor(t[:, BIAS, :], t[:, EXPONENT, :], col_full[:, it.g, :], ALU.mult)\
                    .then_inc(sem("col_bias"), 1)
                dve.wait_ge(sem("rows_taken"), it.of_layer)
                for c in range(C):
                    dve.scalar_tensor_tensor(out=edge[:, c, :], in0=q_rows[:, 1, :], scalar=t[:, R_EIGHTY, c:c + 1],
                                             in1=q_rows[:, 0, :], op0=ALU.subtract, op1=ALU.max)\
                        .then_inc(sem("edge_lin"), 1)

            def weights(it, cs):
                if cs[0] == 0 and (not isinstance(it.g, int) or it.l > 0 or it.g >= 2):
                    dve.wait_ge(sem("att"), it.done - 2)
                for c in cs:
                    dve.wait_ge(sem("edge"), (it.done - 1) * C + (c + 1))
                    m = MT[:, it.g, c, :]
                    if it.l == 1:
                        dve.scalar_tensor_tensor(out=PT[:, it.b, c, :], in0=m, scalar=empty_col[:, it.g, c:c + 1],
                                                 in1=edge[:, c, :], op0=ALU.max, op1=ALU.mult,
                                                 accum_out=col_tmp[:, it.b, Z, c:c + 1]).then_inc(sem("PT"), 1)
                    else:
                        extra = dict(accum_out=col_sum[:, it.b, c:c + 1]) if it.l == 0 else {}
                        dve.scalar_tensor_tensor(out=PT[:, it.b, c, :], in0=edge[:, c, :],
                                                 scalar=factors[:, it.b, 2, c:c + 1], in1=m, op0=ALU.add,
                                                 op1=ALU.mult, **extra).then_inc(sem("PT"), 1)

            def find_empty_columns(it):
                dve.wait_ge(sem("PT"), it.done * C)
                dve.tensor_scalar(empty_col[:, it.g, :], col_sum[:, it.b, :], 0.0, None, ALU.is_equal)\
                    .then_inc(sem("empty_col"), 1)

            def column_sums(it):
                dve.wait_ge(sem("PT"), it.done * C)
                z = col_tmp[:, it.b, Z, :]
                dve.tensor_scalar(z, z, TINY, None, ALU.max).then_inc(sem("z_col"), 1)

            def column_factors(it):
                dve.wait_ge(sem("z_col"), it.of_layer)
                dve.reciprocal(col_tmp[:, it.b, RZ, :], col_tmp[:, it.b, Z, :]).then_inc(sem("rz_col"), 1)

            def row_sums(it):
                dve.wait_ge(sem("att"), it.done)
                dve.tensor_scalar(z_row[:, it.b, :], o_ps[it.b][:, :, 0], TINY, None, ALU.max)\
                    .then_inc(sem("z_row"), 1)

            def row_factors(it):
                dve.wait_ge(sem("z_row"), halves(it))
                dve.reciprocal(rz_row[:, it.b, :], z_row[:, it.b, :]).then_inc(sem("rz_row"), 1)

            def take_out(it):
                o = o_ps[it.b]
                if it.l not in (0, 2):
                    dve.wait_ge(sem("att"), it.done)
                if it.l == 2:
                    dve.wait_ge(sem("y_sum"), it.done - 2)
                elif not isinstance(it.g, int) or it.l > 0 or it.g >= 2:
                    dve.wait_ge(sem("x_new"), it.done - 2)
                if it.l in (0, 2):
                    dve.wait_ge(sem("rz_row"), halves(it))
                    if it.l == 0:
                        dve.wait_ge(sem("residual"), it.done)
                    else:
                        dve.wait_ge(sem("mean_term"), it.of_layer)
                    add, to = (residual, y) if it.l == 0 else (mean_term, lin)
                    for c in range(C):
                        last = dve.scalar_tensor_tensor(out=to[:, it.b, c, :], in0=o[:, c, 1:1 + D],
                                                        scalar=rz_row[:, it.b, c:c + 1], in1=add[:, it.b, c, :],
                                                        op0=ALU.mult, op1=ALU.add)
                    last.then_inc(sem("y_sum" if it.l == 0 else "y_lin"), 1)
                else:
                    dve.wait_ge(sem("residual"), it.of_layer + G)
                    dve.tensor_tensor(y[:, it.b, :, :], o[:, :, 1:1 + D], residual[:, it.b, :, :],
                                      ALU.add).then_inc(sem("y_sum"), 1)

            def add_elu(it):
                dve.wait_ge(sem("elu_low"), it.done - G)
                dve.wait_ge(sem("x_new"), it.done - 2)
                dve.scalar_tensor_tensor(out=y[:, it.b, :, :], in0=lin[:, it.b, :, :], scalar=-1.0,
                                         in1=elu_exp[:, :, :], op0=ALU.max, op1=ALU.add).then_inc(sem("y_sum"), 1)

            def moments(b, y_sem, stats_sem, done):
                dve.wait_ge(y_sem, done)
                for c in range(C):
                    last = dve.bn_stats(stats[:, c, :], y[:, b, c, :])
                last.then_inc(stats_sem, 1)

            def mean_and_variance(b, stats_sem, done, name):
                settle(dve)
                dve.wait_ge(stats_sem, done)
                for c in range(C):
                    last = dve.bn_aggr(mean_var[:, b, c, :], stats[:, c, :])
                last.then_inc(sem(name), 1)

            def finish(it):
                if not isinstance(it.g, int) or it.l > 0 or it.g >= 1:
                    dve.wait_ge(sem("mean_var"), it.done - 1)
                moments(it.b, sem("y_sum"), sem("stats"), it.done)

            def aggregate(it):
                mean_and_variance(it.b, sem("stats"), it.done, "mean_var")

            def rebuild_masks():
                dve.wait_ge(sem("h_ps"), G)
                dve.wait_ge(sem("residual"), G)
                dve.sem_inc(sem("rebuild_taken"), 1)
                with dve.Fori(0, G) as g:
                    dve.wait_ge(sem("rebuild_in"), g * 32 + 32)
                    binary = square_out[:, :].rearrange("p (c i) -> p c i", c=C)
                    for side, empty in enumerate((empty_col, empty_row)):
                        if side:
                            dve.wait_ge(sem("rebuild_count"), g * 2 + 1)
                            dve.wait_ge(sem("rebuild_copied"), g + 1)
                        mark = dve.tensor_scalar(binary, adj_in[:, side, :, :], 0, None, ALU.is_gt)
                        mark.then_inc(sem("rebuild_taken" if side else "rebuild_mask"), 1)
                        if side:
                            dve.wait_ge(sem("rebuild_taken"), g + 2)
                        else:
                            dve.wait_ge(sem("rebuild_mask"), g + 1)
                            dve.tensor_copy(MT[:, g, :, :], binary).then_inc(sem("rebuild_copied"), 1)
                        dve.tensor_reduce(count[:, side, :], binary, AX.X, ALU.add).then_inc(sem("rebuild_count"), 1)
                        dve.wait_ge(sem("rebuild_count"), g * 2 + (side + 1))
                        dve.tensor_scalar(empty[:, g, :], count[:, side, :], 0.0, None, ALU.is_equal)\
                            .then_inc(sem("rebuild_done"), 1)
                dve.wait_ge(sem("rebuild_done"), 2 * G)

            def attention_slot(at, n):
                if n == G - 1:
                    with dve.If(not_binary(dve)):
                        rebuild_masks()
                    dve.wait_ge(sem("empty_col"), G)
                    dve.tensor_scalar(col_full[:, :, :], empty_col[:, :, :], -1.0, 1.0, ALU.mult, ALU.add)\
                        .then_inc(sem("col_full"), 1)
                    dve.wait_ge(sem("col_full"), 1)
                if at(-1) and at(-1).l in (0, 2):
                    row_sums(at(-1))
                if at(2):
                    take_max(at(2))
                if at(-1) and at(-1).l in (0, 2):
                    row_factors(at(-1))
                if at(2):
                    node_shifts(at(2))
                if at(1) and at(1).l == 1:
                    column_terms(at(1))
                if at(2) and at(2).l == 1:
                    exponents(at(2))
                if at(-1) and at(-1).l != 1:
                    take_out(at(-1))
                if at(-2) and at(-2).l == 2:
                    add_elu(at(-2))
                    finish(at(-2))
                if at(1):
                    weights(at(1), (0, 1))
                if at(4) and at(4).l == 0:
                    mask(at(4))
                if at(2) and at(2).l in (0, 2):
                    node_factors(at(2))
                if at(-2) and at(-2).l == 2:
                    aggregate(at(-2))
                if at(-1) and at(-1).l != 2:
                    finish(at(-1))
                if at(1):
                    weights(at(1), (2, 3))
                if at(3):
                    own_max(at(3))
                if at(1) and at(1).l == 1:
                    column_sums(at(1))
                if at(-1) and at(-1).l != 2:
                    aggregate(at(-1))
                if at(1) and at(1).l == 0:
                    find_empty_columns(at(1))
                if at(1) and at(1).l == 1:
                    column_factors(at(1))
                if n == G - 3:
                    dve.wait_ge(sem("flag_sum"), G)
                    dve.tensor_reduce(flag_own[:, 0:1], flag_sum[:, :, 0], AX.X, ALU.max).then_inc(sem("flag_own"), 1)
                    dve.wait_ge(sem("flag_ps"), 1)
                    dve.tensor_reduce(flag_own[:, 1:2], xT_ps[:, 0:P], AX.X, ALU.max).then_inc(sem("flag_max"), 1)
                    dve.wait_ge(sem("flag_max"), 1)
                    dve.tensor_scalar(flag_int[:, :], flag_own[:, 1:2], 0.25 * C * N, None, ALU.is_gt)\
                        .then_inc(sem("flag"), 1)

            def relation_slot(at, n):
                if at(3):
                    it = at(3)
                    dve.wait_ge(sem("split_hi"), it.of_layer)
                    if not isinstance(it.g, int) or it.g >= 1:
                        dve.wait_ge(sem("split"), it.of_layer - 1)
                    dve.tensor_tensor(rest[:, :, :], h_ps[:, :, 0:D], split[:, it.r, 0, :, :], ALU.subtract)\
                        .then_inc(sem("split_rest"), 1)
                if at(-1):
                    take_out(at(-1))
                    finish(at(-1))
                    aggregate(at(-1))
                if at(3):
                    dve.wait_ge(sem("split_mid"), it.of_layer)
                    dve.tensor_tensor(split[:, it.r, 2, :, :], rest[:, :, :], split[:, it.r, 1, :, :], ALU.subtract)\
                        .then_inc(sem("split"), 1)

            pipeline(dve, attention_slot, FIRST, LAST_ATTENTION, G * LAYERS)
            with dve.If(not_binary(dve)):
                pipeline(dve, attention_slot, LAST_ATTENTION, ATTENTION_END, G * LAYERS)
                dve.sem_inc(sem("rel_adj_free"), 1)
                dve.sem_inc(sem("rel_x_new"), 1)
                dve.sem_inc(sem("rel_split_rest"), 1)
                with dve.Fori(0, G) as g:
                    dve.wait_ge(sem("rel_adj_in"), g * 16 + 16)
                    for r in range(REL):
                        n = g * REL + (r + 1)
                        last = dve.tensor_scalar(MT[:, g, :, :], adj_in[:, 0, :, :], r + 1, None, ALU.is_equal)
                        last.then_inc(sem("rel_mask"), 1)
                        dve.wait_ge(sem("rel_split_hi"), n)
                        dve.tensor_tensor(rest[:, :, :], h_ps[:, :, 0:D], split[:, 0, 0, :, :], ALU.subtract)\
                            .then_inc(sem("rel_split_rest"), 1)
                        dve.wait_ge(sem("rel_split_mid"), n)
                        dve.tensor_tensor(split[:, 0, 2, :, :], rest[:, :, :], split[:, 0, 1, :, :], ALU.subtract)\
                            .then_inc(sem("rel_split"), 1)
                        dve.wait_ge(sem("rel_att"), n)
                        if r == 0:
                            dve.wait_ge(sem("rel_residual"), g + 1)
                        else:
                            dve.wait_ge(sem("rel_sum"), g * (REL - 1) + r)
                        dve.tensor_tensor(y[:, 0, :, :], o_ps[0][:, :, 1:1 + D],
                                          residual[:, 0, :, :] if r == 0 else y[:, 0, :, :], ALU.add)\
                            .then_inc(sem("rel_total" if r == REL - 1 else "rel_sum"), 1)
                    dve.wait_ge(sem("rel_mask"), g * REL + REL)
                    dve.sem_inc(sem("rel_adj_free"), 1)
                    moments(0, sem("rel_total"), sem("rel_stats"), g + 1)
                    mean_and_variance(0, sem("rel_stats"), g + 1, "rel_mean_var")
            with dve.Else():
                pipeline(dve, last_layers(attention_slot, relation_slot), LAST_ATTENTION, ALL_STEPS, G * (LAYERS + 1))


def kernel(x, adj, L0_gnn_W, L0_gnn_a, L1_gnn_W, L1_gnn_a, L2_gnn_W_w, L2_gnn_W_b, L2_gnn_ai_w, L2_gnn_ai_b,
           L2_gnn_aj_w, L2_gnn_aj_b, L3_gnn_adj, L3_gnn_weight, L3_gnn_bias):
    import numpy as np
    import concourse.bacc as bacc
    from concourse.bass_utils import run_bass_kernel_spmd

    x, adj = np.asarray(x), np.asarray(adj)
    w0, w1, w2 = (np.asarray(w) for w in (L0_gnn_W, L1_gnn_W, L2_gnn_W_w))
    arrays = {
        "x": x.reshape(G, C, P, D).transpose(0, 2, 1, 3),
        "adj_by_j": adj.transpose(0, 2, 1).reshape(G, C, P, N).transpose(0, 2, 1, 3),
        "adj_by_i": adj.reshape(G, C, P, N).transpose(0, 2, 1, 3),
        "w_by_input": np.stack([w0.T, w1, w2.T], axis=1),
        "w_by_output": np.stack([w0, w1.T, w2], axis=1),
        "a": np.stack([np.asarray(L0_gnn_a).reshape(2, D).T, np.asarray(L1_gnn_a).reshape(2, D).T,
                       np.concatenate([np.asarray(L2_gnn_ai_w), np.asarray(L2_gnn_aj_w)]).T], axis=1),
        "b2": np.asarray(L2_gnn_W_b),
        "ab2": np.concatenate([np.asarray(L2_gnn_ai_b), np.asarray(L2_gnn_aj_b)]),
        "w3": np.asarray(L3_gnn_weight), "b3": np.asarray(L3_gnn_bias),
    }
    arrays = {name: np.ascontiguousarray(a) for name, a in arrays.items()}
    nc = bacc.Bacc("TRN2", target_bir_lowering=False, num_devices=1)
    args = [nc.dram_tensor(name, a.shape, mybir.dt.from_np(a.dtype), kind="ExternalInput").ap()
            for name, a in arrays.items()]
    out = nc.dram_tensor("out", (G, P, C, D), F32, kind="ExternalOutput").ap()
    build(nc, *args, out)
    got = run_bass_kernel_spmd(nc, [arrays], core_ids=[0])
    return np.asarray(got.results[0]["out"]).reshape(G, P, C, D).transpose(0, 2, 1, 3).reshape(G, N, D)
```
